# Optimizing a Trainium2 kernel written in Bass

```python
import numpy as np
import jax
import jax.numpy as jnp

def _softmax(x, axis=-1):
    return jax.nn.softmax(x, axis=axis)

def _gelu(x):
    return jax.nn.gelu(x, approximate=True)

def _silu(x):
    return jax.nn.silu(x)

def _sigmoid(x):
    return jax.nn.sigmoid(x)

def _layernorm(x, axis=-1, eps=1e-05):
    m = jnp.mean(x, axis=axis, keepdims=True)
    v = jnp.var(x, axis=axis, keepdims=True)
    return (x - m) / jnp.sqrt(v + eps)

def _scatter_add(tgt, idx, src, axis=0):
    return tgt.at[idx].add(src)

def _segment_sum(src, seg, n):
    return jax.ops.segment_sum(src, seg, n)
kernel_name = 'mk_audio_tower_d1_tok_audfeat1024_r4_910d22'

def setup_inputs(seed: int=0):
    np.random.seed(seed)
    _w = jnp.asarray

    def _rec_inputs():
        import jax
        import jax.numpy as jnp
        _rk = jax.random.key(seed)
        x = -7.10856e-05 + 0.999911 * jax.random.normal(jax.random.fold_in(_rk, 1), (32, 250, 256), jnp.float32)
        return x
    x = _rec_inputs()

    def _L0_tok_setup():
        import jax, jax.numpy as jnp
        import numpy as np
        N_EMBD = 256
        RF = 2
        FAN_IN = N_EMBD * RF
        EPS = 1e-05
        key = jax.random.key(seed)
        kx, kw, kb = jax.random.split(key, 3)
        x = jax.random.normal(kx, (16, 1024, N_EMBD), dtype=jnp.float32)
        ln_gamma = jnp.ones((FAN_IN,), dtype=jnp.float32)
        ln_beta = jnp.zeros((FAN_IN,), dtype=jnp.float32)
        bound = 1.0 / np.sqrt(FAN_IN)
        W = jax.random.uniform(kw, (N_EMBD, FAN_IN), dtype=jnp.float32, minval=-bound, maxval=bound)
        b = jax.random.uniform(kb, (N_EMBD,), dtype=jnp.float32, minval=-bound, maxval=bound)
        return {'x': x, 'ln_gamma': ln_gamma, 'ln_beta': ln_beta, 'W': W, 'b': b}
    _L0_tok_all = _L0_tok_setup()
    _L0_tok_in = {k: v for k, v in _L0_tok_all.items() if k in ('ln_gamma', 'ln_beta', 'W', 'b')}
    del _L0_tok_all

    def _L0_attn_setup():
        import math
        import jax, jax.numpy as jnp
        import numpy as np
        D, DK, DV = (256, 256, 256)
        B, S = (4, 512)
        key = jax.random.key(seed)
        ks = jax.random.split(key, 4)
        std_qk = math.sqrt(2.0 / (D + DK))
        std_v = math.sqrt(2.0 / (D + DV))
        return {'X': jax.random.normal(ks[0], (B, S, D), dtype=jnp.float32), 'W_q': jax.random.normal(ks[1], (D, DK), dtype=jnp.float32) * std_qk, 'W_k': jax.random.normal(ks[2], (D, DK), dtype=jnp.float32) * std_qk, 'W_v': jax.random.normal(ks[3], (D, DV), dtype=jnp.float32) * std_v, 'b_q': jnp.zeros((DK,), dtype=jnp.float32), 'b_k': jnp.zeros((DK,), dtype=jnp.float32), 'b_v': jnp.zeros((DV,), dtype=jnp.float32)}
    _L0_attn_all = _L0_attn_setup()
    _L0_attn_in = {k: v for k, v in _L0_attn_all.items() if k in ('W_q', 'W_k', 'W_v', 'b_q', 'b_k', 'b_v')}
    del _L0_attn_all

    def _L0_ffn_setup():
        import jax, jax.numpy as jnp
        import numpy as np
        H = 256
        DFF = 1024
        E_ROUTED = 7
        TOP_K = 2

        def _swiglu(flat, gate_w, up_w, down_w):
            g = flat @ gate_w.T
            up = flat @ up_w.T
            return jax.nn.silu(g) * up @ down_w.T
        key = jax.random.key(seed)
        ks = jax.random.split(key, 8)
        s = 0.02
        return {'x': jax.random.normal(ks[0], (4, 512, H), jnp.float32), 'shared_up': jax.random.normal(ks[1], (DFF, H), jnp.float32) * s, 'shared_gate': jax.random.normal(ks[2], (DFF, H), jnp.float32) * s, 'shared_down': jax.random.normal(ks[3], (H, DFF), jnp.float32) * s, 'routed_up': jax.random.normal(ks[4], (E_ROUTED, DFF, H), jnp.float32) * s, 'routed_gate': jax.random.normal(ks[5], (E_ROUTED, DFF, H), jnp.float32) * s, 'routed_down': jax.random.normal(ks[6], (E_ROUTED, H, DFF), jnp.float32) * s, 'router_w': jax.random.normal(ks[7], (E_ROUTED, H), jnp.float32) * 0.02}
    _L0_ffn_all = _L0_ffn_setup()
    _L0_ffn_in = {k: v for k, v in _L0_ffn_all.items() if k in ('shared_up', 'shared_gate', 'shared_down', 'routed_up', 'routed_gate', 'routed_down', 'router_w')}
    del _L0_ffn_all
    return {'x': x, 'L0_tok_ln_gamma': _L0_tok_in['ln_gamma'], 'L0_tok_ln_beta': _L0_tok_in['ln_beta'], 'L0_tok_W': _L0_tok_in['W'], 'L0_tok_b': _L0_tok_in['b'], 'L0_attn_W_q': _L0_attn_in['W_q'], 'L0_attn_W_k': _L0_attn_in['W_k'], 'L0_attn_W_v': _L0_attn_in['W_v'], 'L0_attn_b_q': _L0_attn_in['b_q'], 'L0_attn_b_k': _L0_attn_in['b_k'], 'L0_attn_b_v': _L0_attn_in['b_v'], 'L0_ffn_shared_up': _L0_ffn_in['shared_up'], 'L0_ffn_shared_gate': _L0_ffn_in['shared_gate'], 'L0_ffn_shared_down': _L0_ffn_in['shared_down'], 'L0_ffn_routed_up': _L0_ffn_in['routed_up'], 'L0_ffn_routed_gate': _L0_ffn_in['routed_gate'], 'L0_ffn_routed_down': _L0_ffn_in['routed_down'], 'L0_ffn_router_w': _L0_ffn_in['router_w']}

def reference(x, L0_tok_ln_gamma, L0_tok_ln_beta, L0_tok_W, L0_tok_b, L0_attn_W_q, L0_attn_W_k, L0_attn_W_v, L0_attn_b_q, L0_attn_b_k, L0_attn_b_v, L0_ffn_shared_up, L0_ffn_shared_gate, L0_ffn_shared_down, L0_ffn_routed_up, L0_ffn_routed_gate, L0_ffn_routed_down, L0_ffn_router_w):
    import jax
    import jax.numpy as jnp

    def _L0_tok_ref(x, ln_gamma, ln_beta, W, b):
        import jax, jax.numpy as jnp
        import numpy as np
        N_EMBD = 256
        RF = 2
        FAN_IN = N_EMBD * RF
        EPS = 1e-05
        B, T, C = x.shape
        h = x.reshape(B, T // RF, C * RF)
        mu = jnp.mean(h, axis=-1, keepdims=True)
        var = jnp.mean(jnp.square(h - mu), axis=-1, keepdims=True)
        h = (h - mu) * jax.lax.rsqrt(var + EPS) * ln_gamma + ln_beta
        h = jnp.einsum('btf,ef->bte', h, W) + b
        return jax.nn.relu(h)

    def _L0_attn_ref(X, W_q, W_k, W_v, b_q, b_k, b_v):
        import math
        import jax, jax.numpy as jnp
        import numpy as np
        D, DK, DV = (256, 256, 256)
        B, S = (4, 512)
        scale = 1.0 / math.sqrt(DK)
        Q = X @ W_q + b_q
        K = X @ W_k + b_k
        V = X @ W_v + b_v
        A = jnp.einsum('bsd,btd->bst', Q, K) * scale
        A = jax.nn.softmax(A, axis=2)
        return jnp.einsum('bst,btv->bsv', A, V)

    def _L0_ffn_ref(x, shared_up, shared_gate, shared_down, routed_up, routed_gate, routed_down, router_w):
        import jax, jax.numpy as jnp
        import numpy as np
        H = 256
        DFF = 1024
        E_ROUTED = 7
        TOP_K = 2

        def _swiglu(flat, gate_w, up_w, down_w):
            g = flat @ gate_w.T
            up = flat @ up_w.T
            return jax.nn.silu(g) * up @ down_w.T
        orig_shape = x.shape
        flat = x.reshape(-1, H)
        out = _swiglu(flat, shared_gate, shared_up, shared_down)
        logits = flat @ router_w.T
        probs = jax.nn.softmax(logits, axis=-1)
        top_vals, top_idx = jax.lax.top_k(probs, TOP_K)
        top_vals = top_vals / (top_vals.sum(-1, keepdims=True) + 1e-09)
        combine = jnp.sum(jax.nn.one_hot(top_idx, E_ROUTED, dtype=flat.dtype) * top_vals[..., None], axis=1)
        routed = jnp.zeros_like(flat)
        for e in range(E_ROUTED):
            eo = _swiglu(flat, routed_gate[e], routed_up[e], routed_down[e])
            routed = routed + combine[:, e:e + 1] * eo
        return (out + routed).reshape(orig_shape)
    h = _L0_tok_ref(x, L0_tok_ln_gamma, L0_tok_ln_beta, L0_tok_W, L0_tok_b)
    h = h + _L0_attn_ref(_layernorm(h, axis=-1), L0_attn_W_q, L0_attn_W_k, L0_attn_W_v, L0_attn_b_q, L0_attn_b_k, L0_attn_b_v)
    h = h + _L0_ffn_ref(_layernorm(h, axis=-1), L0_ffn_shared_up, L0_ffn_shared_gate, L0_ffn_shared_down, L0_ffn_routed_up, L0_ffn_routed_gate, L0_ffn_routed_down, L0_ffn_router_w)
    return h

_drawn_inputs = setup_inputs


def setup_inputs(seed=0):
    import zlib

    import numpy as np

    out = dict(_drawn_inputs(seed))
    spreads = {'L0_tok_ln_gamma': (1.0, 0.2),
     'L0_tok_ln_beta': (0.0, 0.1),
     'L0_attn_b_q': (0.0, 0.284),
     'L0_attn_b_k': (0.0, 0.8),
     'L0_attn_b_v': (0.0, 0.1)}
    factors = {}
    for name, (base, spread) in spreads.items():
        noise = np.random.default_rng([zlib.crc32(name.encode()), seed]).standard_normal(out[name].shape)
        drawn = base * np.exp(spread * noise) if base else spread * noise
        out[name] = jnp.asarray(drawn.astype(out[name].dtype))
    for name, factor in factors.items():
        out[name] = (out[name] * factor).astype(out[name].dtype)
    return out
```

```python
from contextlib import ExitStack

import concourse.bass as bass
from concourse import mybir

F32 = mybir.dt.float32
BF16 = mybir.dt.bfloat16
I32 = mybir.dt.int32
ALU = mybir.AluOpType
ACT = mybir.ActivationFunctionType
AX = mybir.AxisListType.X

P = 128
B, T_IN, C = 32, 250, 256
FAN = 2 * C
S = T_IN // 2
NTOK = B * S
D = 256
DC = D // P
FC = FAN // P
DFF = 1024
HC = DFF // P
E = 7
NE = E + 1
GS = 4
NG = B // GS
GT = GS * S

TILE = 256
SUB = TILE // P
NT = (2 * NTOK + E * (TILE - 1)) // TILE
REGION = 4096
TABLE = (E - 1) * REGION + NT * TILE
NS = 3
PART = 2048
SLOT = 3 * 2 * PART
EPS = 1e-5
RSQRT_SEED = float(0x5F3759DF)

assert NT % 2 == 0 and NTOK <= REGION and TABLE % P == 0 and NG == E + 1


def audio_tower(nc, x, columns, w_tok, b_tok, w_qkv, b_v, w_ffn, w_router, out):
    with ExitStack() as ctx:
        def sb(name, shape, dt=F32):
            return ctx.enter_context(nc.sbuf_tensor(name, shape, dt))

        def bank(name):
            return ctx.enter_context(nc.psum_tensor(name, [P, 512], F32))

        def sem(name):
            return ctx.enter_context(nc.semaphore(name))

        token_rows = nc.dram_tensor("token_rows", [NTOK, 2 * D], BF16).ap()
        choices = nc.dram_tensor("choices", [TABLE, 2], I32).ap()
        split_ffn = nc.dram_tensor("split_ffn", [E, 3, P, 2 * PART], BF16).ap()

        ident = sb("ident", [P, P])
        ident_b = sb("ident_b", [P, P], BF16)
        before = sb("before", [P, P], BF16)
        ones_b = sb("ones_b", [P, P], BF16)
        wtok = sb("wtok", [P, FC, D])
        wqkv = sb("wqkv", [P, 3, DC, D])
        wrt = sb("wrt", [P, DC, E])
        cols = sb("cols", [P, 2 * FC + 2 * DC])
        gam, bet = cols[:, 0:FC], cols[:, FC:2 * FC]
        bqk = cols[:, 2 * FC:].rearrange("p (w c) -> p w c", w=2)
        btok2 = sb("btok2", [P, 2, D])
        bv2 = sb("bv2", [P, 2, D])
        prio = sb("prio", [P, E])
        base_e = sb("base_e", [P, E])
        tokid = sb("tokid", [P, GS])
        iota_i = sb("iota_i", [P, 64], I32)
        tile_no = sb("tile_no", [P, NT])

        xin = sb("xin", [P, GS, FAN])
        yT = sb("yT", [P, FC, GT])
        hpre = sb("hpre", [P, GS, D])
        h = sb("h", [P, GS, D])
        xn = sb("xn", [P, GS, D])
        xnT = sb("xnT", [P, DC, GT])
        qT = sb("qT", [P, DC, GT])
        kT = sb("kT", [P, DC, GT])
        v = sb("v", [P, GS, D])
        prob = sb("prob", [P, GS, S])
        probT = sb("probT", [P, GS, S])
        h2 = hpre
        stats = sb("stats", [P, GS, 6])
        mv = sb("mv", [P, GS, 2])
        ve = sb("ve", [P, GS])
        hv = sb("hv", [P, GS])
        rs = sb("rs", [P, GS])
        sq = sb("sq", [P, GS])
        smax = sb("smax", [P, GS])
        ssum = sb("ssum", [P, GS])
        logT = sb("logT", [E, GT])
        lg = sb("lg", [P, GS, E])
        pr = sb("pr", [P, GS, E])
        t7 = sb("t7", [P, GS, E])
        oh1 = sb("oh1", [P, GS, E])
        oh2 = sb("oh2", [P, GS, E])
        pick = sb("pick", [P, GS, E], BF16)
        run = sb("run", [P, GS + 1, E])
        m1 = sb("m1", [P, GS])
        m2 = sb("m2", [P, GS])
        r1 = sb("r1", [P, GS])
        posf = sb("posf", [P, GS, 2])
        pos = sb("pos", [P, GS, 2], I32)
        meta = sb("meta", [P, GS, 2, 2], I32)
        rows = sb("rows", [P, GS, 2 * D], BF16)
        x2T = sb("x2T", [P, 2, DC, GT], BF16)
        hres = sb("hres", [P, GS, D])
        yout = sb("yout", [P, GS, D])
        hid = sb("hid", [P, 2, HC, 512], BF16)
        hidr = hid[:].rearrange("p a c (b t) -> p b a c t", b=2)
        sil = sb("sil", [P, 2, 512])
        stage = sb("stage", [P, PART])
        split = sb("split", [P, 2, PART], BF16)
        W = sb("W", [P, NS * SLOT], BF16)
        grow = sb("grow", [P, 2, SUB, 2 * D], BF16)
        gxT = sb("gxT", [P, 2, 2, DC, TILE], BF16)
        gmeta = sb("gmeta", [P, 2, SUB, 2], I32)
        smeta = sb("smeta", [P, 2, SUB, 2], I32)
        gidx = sb("gidx", [P, 2, SUB], I32)
        ysb = sb("ysb", [P, 2, SUB, D])
        ntile = sb("ntile", [1, E], I32)
        tends = sb("tends", [1, E])
        tcount = sb("tcount", [1, E])
        ends_i = sb("ends_i", [1, 8], I32)
        passed = sb("passed", [1, NT, E])
        ej = sb("ej", [1, NT])
        sj = sb("sj", [1, NT])
        tj = sb("tj", [1, NT])
        plan = sb("plan", [1, 3, NT], I32)
        padfill = grow[:].rearrange("p a b c -> p (a b c)").bitcast(I32)[:, 0:TABLE // P * 2].rearrange("p (r w) -> p r w", w=2)

        psT, psA0, psA1, psY = bank("psT"), bank("psA0"), bank("psA1"), bank("psY")
        psG = [bank("psG0"), bank("psG1")]
        psU = [bank("psU0"), bank("psU1")]
        psA = [psA0, psA1]
        psT_b = psT[:, :].bitcast(BF16)

        T_full, T_free = sem("T_full"), sem("T_free")
        A_full, A_free = [sem("A0_full"), sem("A1_full")], [sem("A0_free"), sem("A1_free")]
        Y_full, Y_free = sem("Y_full"), sem("Y_free")
        G_full, G_free = [sem("G0_full"), sem("G1_full")], [sem("G0_free"), sem("G1_free")]
        U_full = [sem("U0_full"), sem("U1_full")]
        T_X, T_XN, T_SC, T_X2, T_LG, T_USES = 0, FC, FC + 2, FC + 3, FC + 5, FC + 6
        A_TOK, A_Q, A_K, A_V, A0_PT, A0_PV, A0_RANK = range(7)
        A1_PV, A1_LG = 4, 5
        A_USES = [7, 6]
        G_USES, U_USES, Y_USES = [HC // 2 + 2, HC // 2], HC // 2, 2

        consts_loaded, masks_made, biases_loaded = sem("consts_loaded"), sem("masks_made"), sem("biases_loaded")
        iota_made, indices_made = sem("iota_made"), sem("indices_made")
        pads_masked, pads_made, pads_stored = sem("pads_masked"), sem("pads_made"), sem("pads_stored")
        x_loaded, xhat_ready = sem("x_loaded"), sem("xhat_ready")
        h_ready, xn_ready = sem("h_ready"), sem("xn_ready")
        smax_ready = sem("smax_ready")
        hres_ready, xn2_ready = sem("hres_ready"), sem("xn2_ready")
        rows_hi, rows_lo, rows_stored = sem("rows_hi"), sem("rows_lo"), sem("rows_stored")
        x2_f32, x2_hi, x2_lo = sem("x2_f32"), sem("x2_hi"), sem("x2_lo")
        e_ready = sem("e_ready")
        pick_ready, meta_ready, meta_stored = sem("pick_ready"), sem("meta_ready"), sem("meta_stored")
        dve_step, passed_by = sem("dve_step"), sem("passed_by")
        sil_ready, hf_ready, hid_hi, hid_lo = sem("sil_ready"), sem("hf_ready"), sem("hid_hi"), sem("hid_lo")
        out_stored = sem("out_stored")
        stage_loaded, split_hi, split_lo, split_stored = (
            sem("stage_loaded"), sem("split_hi"), sem("split_lo"), sem("split_stored"))
        plan_ready, expert_loaded = sem("plan_ready"), sem("expert_loaded")
        gmeta_loaded, gidx_ready, grow_loaded = sem("gmeta_loaded"), sem("gidx_ready"), sem("grow_loaded")
        smeta_ready, added = sem("smeta_ready"), sem("added")

        def at(g, per_group, n):
            return g * per_group + n

        def wait_apart(eng, sem, value):
            eng.wait_ge(sem, value).then_inc(passed_by, 1)

        def wcols(slot_at, which, part, first, n):
            return W[:, bass.ds(slot_at + (2 * which + part) * PART + first, n)]

        TERMS = ((0, 0), (0, 1), (1, 0))
        x_groups = x.rearrange("(g s) p f -> g p s f", s=GS)
        out_groups = out[0:NTOK, :].rearrange("(g s p) d -> g p s d", s=GS, p=S)
        rows_groups = token_rows.rearrange("(g s p) d -> g p s d", s=GS, p=S)
        w_stage = w_ffn.rearrange("e t p n -> (e t) p n")
        split_steps = split_ffn.rearrange("e t p n -> (e t) p n")
        choice_tiles = choices.rearrange("(r p k) w -> r p (k w)", p=P, k=SUB)

        block = ctx.enter_context(nc.Block())

        @block.sync
        def _(sp):
            def load_stage(step):
                sp.dma_start(stage[:, :], w_stage[step, :, :]).then_inc(stage_loaded, 16)

            def load_x(g):
                sp.dma_start(xin[0:S, :, :], x_groups[g, :, :, :]).then_inc(x_loaded, 16)

            def split_traffic(g, first):
                for t in range(3):
                    sp.wait_ge(split_lo, at(g, 3, t + 1))
                    load_stage(g * 3 + t + 1)
                    if not first:
                        sp.dma_start(split_steps[(g - 1) * 3 + t, :, :],
                                     split[:, :, :].rearrange("p a n -> p (a n)")).then_inc(split_stored, 16)

            load_x(0)
            load_stage(0)
            sp.dma_start(wtok[:, :, :], w_tok.rearrange("(c p) n -> p c n", p=P)).then_inc(consts_loaded, 16)
            sp.dma_start(wqkv[:, :, :, :], w_qkv.rearrange("w (c p) n -> p w c n", p=P)).then_inc(consts_loaded, 16)
            sp.dma_start(wrt[:, :, :], w_router.rearrange("(c p) n -> p c n", p=P)).then_inc(consts_loaded, 16)

            def rest_of_group(g, first):
                sp.wait_ge(T_full, at(g, T_USES, T_X + FC))
                load_x(g + 1)
                split_traffic(g, first)
                sp.wait_ge(rows_hi, at(g, 1, 1))
                sp.wait_ge(rows_lo, at(g, 1, 1))
                sp.dma_start(rows_groups[g, :, :, :], rows[0:S, :, :]).then_inc(rows_stored, 16)

            def store_out(g):
                sp.wait_ge(Y_free, at(g, Y_USES, Y_USES))
                sp.wait_ge(G_free[0], at(g, G_USES[0], G_USES[0]))
                sp.dma_start(out_groups[g, :, :, :], yout[0:S, :, :]).then_inc(out_stored, 16)

            rest_of_group(0, True)
            rest_of_group(1, False)
            store_out(0)
            with sp.Fori(2, NG - 1) as g:
                rest_of_group(g, False)
                store_out(g - 1)
            for t in range(3):
                sp.wait_ge(split_lo, (NG - 1) * 3 + t + 1)
                if t < 2:
                    load_stage((NG - 1) * 3 + t + 1)
                sp.dma_start(split_steps[(NG - 2) * 3 + t, :, :],
                             split[:, :, :].rearrange("p a n -> p (a n)")).then_inc(split_stored, 16)
            sp.wait_ge(rows_hi, NG)
            sp.wait_ge(rows_lo, NG)
            sp.dma_start(rows_groups[NG - 1, :, :, :], rows[0:S, :, :]).then_inc(rows_stored, 16)
            store_out(NG - 2)

            sp.wait_ge(split_stored, 16 * 3 * E)
            for n in range(1, NE):
                if n == NS:
                    store_out(NG - 1)
                if n == NS + 1:
                    sp.wait_ge(plan_ready, 1)
                if n > NS:
                    ended = sp.value_load(ends_i[0:1, n - NS - 1:n - NS], min_val=0, max_val=NT)
                    sp.wait_ge(Y_full, ended * SUB + NG * Y_USES)
                sp.dma_start(
                    W[:, (n % NS) * SLOT:(n % NS + 1) * SLOT].rearrange("p (t n) -> p t n", t=3),
                    split_ffn[n - 1, :, :, :].rearrange("t p n -> p t n")).then_inc(expert_loaded, 16)
                sp.wait_ge(expert_loaded, 16 * n)
            sp.wait_ge(out_stored, 16 * NG)
            sp.wait_ge(added, 16 * SUB * NT)

        @block.gpsimd
        def _(pool):
            def iota(dst, pattern, base, mult):
                pool.iota(dst, pattern, base=base, channel_multiplier=mult).then_inc(iota_made, 1)

            pool.memset(ident[:, :], 0.0).then_inc(masks_made, 1)
            pool.memset(before[:, :], 1.0).then_inc(masks_made, 1)
            pool.memset(ones_b[:, :], 1.0).then_inc(masks_made, 1)
            pool.memset(yout[:, 0:2, :], 0.0).then_inc(pads_made, 1)
            pool.memset(padfill[:, :, 1], 0).then_inc(pads_made, 1)
            iota(padfill[:, :, 0], [[1, TABLE // P]], 0, TABLE // P)
            iota(iota_i[:, 0:E], [[-1, E]], E, 0)
            iota(iota_i[:, 8:8 + E], [[REGION, E]], 0, 0)
            iota(iota_i[:, 16:16 + GS], [[S, GS]], 0, 1)
            iota(iota_i[:, 20:20 + NT], [[1, NT]], 0, 0)
            pool.wait_ge(pads_made, 3)
            pool.dma_start(choices.rearrange("(p r) w -> p r w", p=P), padfill).then_inc(pads_stored, 16)
            pool.dma_start(out[NTOK:NTOK + TILE, :].rearrange("(k p) d -> p k d", p=P), yout[:, 0:2, :]
                           ).then_inc(pads_stored, 16)
            pool.wait_ge(masks_made, 3)
            pool.affine_select(out=ident[:, :], in_=ident[:, :], compare_op=ALU.not_equal, fill=1.0, base=0,
                               pattern=[[-1, P]], channel_multiplier=1).then_inc(masks_made, 1)
            pool.affine_select(out=before[:, :], in_=before[:, :], compare_op=ALU.is_gt, fill=0.0, base=0,
                               pattern=[[1, P]], channel_multiplier=-1).then_inc(masks_made, 1)
            pool.wait_ge(masks_made, 5)
            pool.tensor_copy(ident_b[:, :], ident[:, :]).then_inc(masks_made, 1)
            pool.wait_ge(pads_stored, 32)

            def residual(g, first):
                wait_apart(pool, A_free[0], at(g, A_USES[0], A0_PV + 1))
                if not first:
                    wait_apart(pool, G_free[0], at(g - 1, G_USES[0], G_USES[0]))
                pool.tensor_copy(hres[0:S, :, :], h2[0:S, :, :]).then_inc(hres_ready, 1)

            def store_choices(g):
                wait_apart(pool, meta_ready, at(g, 1, 1))
                for s in range(GS):
                    for k in range(2):
                        pool.indirect_dma_start(
                            choices[:, :], bass.IndirectOffsetOnAxis(ap=pos[0:S, s, k:k + 1], axis=0),
                            meta[0:S, s, k, :], None).then_inc(meta_stored, 16)

            residual(0, True)
            store_choices(0)
            residual(1, False)
            store_choices(1)
            with pool.Fori(2, NG) as g:
                residual(g, False)
                store_choices(g)

            pool.wait_ge(plan_ready, 1)
            pool.wait_ge(meta_stored, 16 * 2 * GS * NG)
            pool.wait_ge(rows_stored, 16 * NG)

            def load_choices(j, b):
                row = pool.value_load(plan[0:1, 2, bass.ds(j, 1)], min_val=0, max_val=TABLE // TILE - 1)
                pool.dma_start(gmeta[:, b, :, :].rearrange("p k w -> p (k w)"),
                               choice_tiles[bass.ds(row, 1), :, :].rearrange("r p n -> (r p) n")
                               ).then_inc(gmeta_loaded, 16)
                wait_apart(pool, gmeta_loaded, at(j, 16, 16))
                pool.tensor_scalar(gidx[:, b, :], gmeta[:, b, :, 0], NTOK - 1, None, ALU.min).then_inc(gidx_ready, 1)
                wait_apart(pool, gidx_ready, at(j, 1, 1))

            def gather_rows(j, b):
                for k in range(SUB):
                    pool.indirect_dma_start(
                        grow[:, b, k, :], None, token_rows[:, :],
                        bass.IndirectOffsetOnAxis(ap=gidx[:, b, k:k + 1], axis=0)).then_inc(grow_loaded, 16)

            def keep_meta(j, b):
                pool.tensor_copy(smeta[:, b, :, :], gmeta[:, b, :, :]).then_inc(smeta_ready, 1)

            def add_rows(j, b):
                wait_apart(pool, Y_free, at(j, SUB, SUB) + NG * Y_USES)
                for k in range(SUB):
                    pool.indirect_dma_start(
                        out[:, :], bass.IndirectOffsetOnAxis(ap=smeta[:, b, k, 0:1], axis=0),
                        ysb[:, b, k, :], None, compute_op=ALU.add).then_inc(added, 16)

            def tile_steps(j, b, older, newer):
                if older >= 2:
                    wait_apart(pool, added, at(j - 1, 16 * SUB, 0))
                keep_meta(j, b)
                if newer:
                    pool.wait_ge(smeta_ready, at(j, 1, 1))
                    load_choices(j + 2, b)
                    wait_apart(pool, T_full, at(j, 1, 1) + NG * T_USES)
                    gather_rows(j + 2, b)
                if older >= 1:
                    add_rows(j - 1, 1 - b)

            for b in range(2):
                load_choices(b, b)
                gather_rows(b, b)
                pool.wait_ge(grow_loaded, 16 * SUB * (b + 1))
            tile_steps(0, 0, 0, True)
            pool.wait_ge(out_stored, 16 * NG)
            tile_steps(1, 1, 1, True)
            with pool.Fori(1, NT // 2 - 1) as i:
                for b in range(2):
                    tile_steps(i * 2 + b, b, 2, True)
            for b in range(2):
                tile_steps(NT - 2 + b, b, 2, False)
            pool.wait_ge(added, 16 * SUB * (NT - 1))
            add_rows(NT - 1, 1)
            pool.wait_ge(added, 16 * SUB * NT)

        @block.scalar
        def _(act):
            act.dma_start(cols[:, :], columns).then_inc(biases_loaded, 16)
            for s in range(2):
                act.dma_start(btok2[:, s, :], b_tok.partition_broadcast(P)).then_inc(biases_loaded, 16)
                act.dma_start(bv2[:, s, :], b_v.partition_broadcast(P)).then_inc(biases_loaded, 16)
            act.wait_ge(biases_loaded, 16 * 5)

            def split_high(g, t, first):
                act.wait_ge(stage_loaded, at(g, 48, 16 * (t + 1)))
                if first:
                    dst = W[:, 2 * t * PART:(2 * t + 1) * PART]
                else:
                    act.wait_ge(split_stored, at(g - 1, 48, 16 * t))
                    dst = split[:, 0, :]
                act.activation(dst, stage[:, :], ACT.Copy).then_inc(split_hi, 1)

            def token_inputs(g, k):
                act.wait_ge(T_full, at(g, T_USES, T_X + k + 1))
                act.activation(yT[:, k, :], psT[:, 0:GT], ACT.Identity, bias=bet[:, k:k + 1],
                               scale=gam[:, k:k + 1]).then_inc(T_free, 1)

            def relu(g):
                for a in range(2):
                    act.wait_ge(A_free[a], at(g, A_USES[a], A_TOK + 1))
                act.activation(h[0:S, :, :], hpre[0:S, :, :], ACT.Relu).then_inc(h_ready, 1)

            def normed_T(g, k):
                act.wait_ge(T_full, at(g, T_USES, T_XN + k + 1))
                act.activation(xnT[:, k, :], psT[:, 0:GT], ACT.Copy).then_inc(T_free, 1)

            def queries_keys(g, w):
                for m in range(DC):
                    act.wait_ge(A_full[m], at(g, A_USES[m], A_Q + w + 1))
                    act.activation((qT, kT)[w][:, m, :], psA[m][:, 0:GT], ACT.Identity,
                                   bias=bqk[:, w, m:m + 1]).then_inc(A_free[m], 1)

            def exps(g):
                act.wait_ge(smax_ready, at(g, 1, 1))
                for s in range(GS):
                    last = act.activation(prob[0:S, s, :], psT[0:S, s * S:(s + 1) * S], ACT.Exp,
                                          bias=smax[0:S, s:s + 1], scale=D ** -0.5, accum_out=ssum[0:S, s:s + 1])
                last.then_inc(T_free, 1)

            def token_rows_high(g):
                act.wait_ge(xn2_ready, at(g, 1, 1))
                act.wait_ge(rows_stored, at(g, 16, 0))
                act.activation(rows[0:S, :, 0:D], xn[0:S, :, :], ACT.Copy).then_inc(rows_hi, 1)

            def ffn_inputs(g):
                for k in range(DC):
                    act.wait_ge(T_full, at(g, T_USES, T_X2 + k + 1))
                    act.activation(xnT[:, k, :], psT[:, 0:GT], ACT.Copy).then_inc(T_free, 1)
                for k in range(DC):
                    act.wait_ge(T_free, at(g, T_USES, T_X2 + k + 1))
                    act.activation(x2T[:, 0, k, :], xnT[:, k, :], ACT.Copy).then_inc(x2_hi, 1)

            def router(g):
                act.wait_ge(T_full, at(g, T_USES, T_LG + 1))
                act.activation(logT[:, :], psT[0:E, 0:GT], ACT.Copy).then_inc(T_free, 1)
                act.wait_ge(A_free[1], at(g, A_USES[1], A1_LG + 1))
                act.activation(pr[0:S, :, :], lg[0:S, :, :], ACT.Exp).then_inc(e_ready, 1)

            def ffn_piece(g, c):
                if c < HC:
                    act.wait_ge(G_full[c % 2], at(g, G_USES[c % 2], c // 2 + 1))
                    act.wait_ge(hid_lo, at(g, HC, max(c - 1, 0)))
                    act.activation(sil[:, c % 2, 0:GT], psG[c % 2][:, 0:GT], ACT.Silu).then_inc(G_free[c % 2], 1)
                if c >= 1:
                    act.wait_ge(hf_ready, at(g, HC, c))
                    if c == 1:
                        act.wait_ge(G_free[0], at(g, G_USES[0], 0))
                    act.activation(hid[:, 0, c - 1, 0:GT], sil[:, (c - 1) % 2, 0:GT], ACT.Copy).then_inc(hid_hi, 1)

            def group(g, first):
                ffn = (lambda c: None) if first else (lambda c: ffn_piece(g - 1, c))
                ffn(0)
                ffn(1)
                split_high(g, 0, first)
                token_inputs(g, 0)
                token_inputs(g, 1)
                ffn(2)
                token_inputs(g, 2)
                token_inputs(g, 3)
                ffn(3)
                split_high(g, 1, first)
                ffn(4)
                relu(g)
                ffn(5)
                split_high(g, 2, first)
                normed_T(g, 0)
                ffn(6)
                normed_T(g, 1)
                queries_keys(g, 0)
                queries_keys(g, 1)
                ffn(7)
                ffn(8)
                exps(g)
                token_rows_high(g)
                ffn_inputs(g)
                router(g)

            group(0, True)
            group(1, False)
            with act.Fori(2, NG) as g:
                group(g, False)
            for c in range(HC + 1):
                ffn_piece(NG - 1, c)

            def routed_tile(j, b, first):
                Q = HC // 2
                for q in range(Q + 1):
                    if q < Q:
                        act.wait_ge(G_full[q % 2], at(j, Q // 2, q // 2 + 1) + NG * G_USES[q % 2])
                        act.wait_ge(hid_lo, at(j, Q, max(q - 1, 0)) + NG * HC)
                        act.activation(sil[:, q % 2, :], psG[q % 2][:, :], ACT.Silu).then_inc(G_free[q % 2], 1)
                    if q >= 1:
                        act.wait_ge(hf_ready, at(j, Q, q) + NG * HC)
                        if q == 1 and first:
                            act.wait_ge(G_free[0], NG * G_USES[0])
                        elif q == 1:
                            act.wait_ge(Y_full, (j - 1) * SUB + NG * Y_USES)
                        act.activation(hidr[:, b, 0, 2 * q - 2:2 * q, :],
                                       sil[:, (q - 1) % 2, :].rearrange("p (c t) -> p c t", c=2),
                                       ACT.Copy).then_inc(hid_hi, 1)

            for b in range(2):
                routed_tile(b, b, True)
            with act.Fori(1, NT // 2) as i:
                for b in range(2):
                    routed_tile(i * 2 + b, b, False)

        @block.vector
        def _(vec):
            vec.wait_ge(iota_made, 5)
            vec.tensor_scalar(padfill[:, :, 0], padfill[:, :, 0], TILE - 1, None, ALU.bitwise_and
                              ).then_inc(pads_masked, 1)
            vec.wait_ge(pads_masked, 1)
            vec.tensor_scalar(padfill[:, :, 0], padfill[:, :, 0], NTOK, None, ALU.add).then_inc(pads_made, 1)
            vec.tensor_copy(prio[:, :], iota_i[:, 0:E])
            vec.tensor_copy(base_e[:, :], iota_i[:, 8:8 + E])
            vec.tensor_copy(run[:, 0, :], iota_i[:, 8:8 + E])
            vec.tensor_copy(tokid[:, :], iota_i[:, 16:16 + GS])
            vec.tensor_copy(tile_no[:, :], iota_i[:, 20:20 + NT]).then_inc(indices_made, 1)
            vec.wait_ge(masks_made, 6)
            vec.wait_ge(indices_made, 1)
            vec.wait_ge(biases_loaded, 16 * 5)

            STEPS = 70
            state = {"g": 0, "n": 0}

            def link(ins, wait=lambda eng, sem, value: eng.wait_ge(sem, value)):
                state["n"] += 1
                ins.then_inc(dve_step, 1)
                wait(vec, dve_step, at(state["g"], STEPS, state["n"]))

            def bc(ap, n):
                return ap.unsqueeze(2).to_broadcast([S, GS, n])

            def norm(src, dst, done):
                for s in range(GS):
                    last = vec.bn_stats(stats[0:S, s, :], src[0:S, s, :])
                link(last, wait_apart)
                for s in range(GS):
                    last = vec.bn_aggr(mv[0:S, s, :], stats[0:S, s, :])
                link(last)
                link(vec.tensor_scalar(ve[0:S, :], mv[0:S, :, 1], EPS, None, ALU.add))
                vec.tensor_scalar(hv[0:S, :], ve[0:S, :], -0.5, None, ALU.mult)
                link(vec.tensor_scalar(rs[0:S, :].bitcast(I32), ve[0:S, :].bitcast(I32), -0.5, RSQRT_SEED,
                                       ALU.mult, ALU.add))
                for _ in range(3):
                    link(vec.tensor_tensor(sq[0:S, :], rs[0:S, :], rs[0:S, :], ALU.mult))
                    link(vec.tensor_tensor(sq[0:S, :], sq[0:S, :], hv[0:S, :], ALU.mult))
                    link(vec.scalar_tensor_tensor(rs[0:S, :], sq[0:S, :], 1.5, rs[0:S, :], ALU.add, ALU.mult))
                for s in range(GS):
                    last = vec.tensor_scalar(dst[0:S, s, :], src[0:S, s, :], mv[0:S, s, 0:1], rs[0:S, s:s + 1],
                                             ALU.subtract, ALU.mult)
                last.then_inc(done, 1)

            def split_low(g, t, first):
                vec.wait_ge(split_hi, at(g, 3, t + 1))
                if first:
                    hi = W[:, 2 * t * PART:(2 * t + 1) * PART]
                    lo = W[:, (2 * t + 1) * PART:(2 * t + 2) * PART]
                else:
                    hi, lo = split[:, 0, :], split[:, 1, :]
                vec.tensor_tensor(lo, stage[:, :], hi, ALU.subtract).then_inc(split_lo, 1)

            def project_bias(g):
                for a in range(2):
                    vec.wait_ge(A_full[a], at(g, A_USES[a], A_TOK + 1))
                    if a == 0:
                        vec.wait_ge(hres_ready, at(g, 1, 0))
                    vec.tensor_tensor(hpre[0:S, 2 * a:2 * a + 2, :].rearrange("p s d -> p (s d)"),
                                      psA[a][0:S, :], btok2[0:S, :, :].rearrange("p s d -> p (s d)"),
                                      ALU.add).then_inc(A_free[a], 1)

            def values(g):
                for a in range(2):
                    vec.wait_ge(A_full[a], at(g, A_USES[a], A_V + 1))
                    vec.tensor_tensor(v[0:S, 2 * a:2 * a + 2, :].rearrange("p s d -> p (s d)"),
                                      psA[a][0:S, :], bv2[0:S, :, :].rearrange("p s d -> p (s d)"),
                                      ALU.add).then_inc(A_free[a], 1)

            def score_max(g):
                vec.wait_ge(T_full, at(g, T_USES, T_SC + 1))
                link(vec.tensor_reduce(smax[0:S, :], psT[0:S, 0:GT].rearrange("p (s t) -> p s t", s=GS),
                                       AX, ALU.max))
                vec.tensor_scalar(smax[0:S, :], smax[0:S, :], -D ** -0.5, None, ALU.mult).then_inc(smax_ready, 1)

            def probs_T(g):
                vec.wait_ge(A_full[0], at(g, A_USES[0], A0_PT + 1))
                vec.tensor_copy(probT[0:S, :, :].rearrange("p s t -> p (s t)"), psA[0][0:S, 0:GT]
                                ).then_inc(A_free[0], 1)
                vec.wait_ge(T_free, at(g, T_USES, T_SC + 1))
                link(vec.reciprocal(ssum[0:S, :], ssum[0:S, :]))

            def attended(g):
                for a, use in ((1, A1_PV), (0, A0_PV)):
                    vec.wait_ge(A_full[a], at(g, A_USES[a], use + 1))
                    for i in range(2):
                        s = 2 * (1 - a) + i
                        last = vec.scalar_tensor_tensor(h2[0:S, s, :], psA[a][0:S, i * D:(i + 1) * D],
                                                        ssum[0:S, s:s + 1], h[0:S, s, :], ALU.mult, ALU.add)
                    last.then_inc(A_free[a], 1)
                vec.wait_ge(A_free[0], at(g, A_USES[0], A0_PV + 1))

            def token_rows_low(g):
                vec.wait_ge(rows_hi, at(g, 1, 1))
                vec.tensor_tensor(rows[0:S, :, D:2 * D], xn[0:S, :, :], rows[0:S, :, 0:D], ALU.subtract
                                  ).then_inc(rows_lo, 1)

            def ffn_inputs_low(g):
                for k in range(DC):
                    vec.wait_ge(x2_hi, at(g, DC, k + 1))
                    vec.tensor_tensor(x2T[:, 1, k, :], xnT[:, k, :], x2T[:, 0, k, :], ALU.subtract
                                      ).then_inc(x2_lo, 1)

            def top2(g):
                vec.wait_ge(A_full[1], at(g, A_USES[1], A1_LG + 1))
                logits = psA[1][0:S, 0:GS * 8].rearrange("p (s e) -> p s e", e=8)[:, :, 0:E]
                link(vec.tensor_reduce(m1[0:S, :], logits, AX, ALU.max))
                vec.tensor_tensor(lg[0:S, :, :], logits, bc(m1[0:S, :], E), ALU.subtract).then_inc(A_free[1], 1)
                vec.wait_ge(e_ready, at(g, 1, 1))
                link(vec.tensor_reduce(r1[0:S, :], pr[0:S, :, :], AX, ALU.add))
                link(vec.reciprocal(r1[0:S, :], r1[0:S, :]))
                link(vec.tensor_tensor(pr[0:S, :, :], pr[0:S, :, :], bc(r1[0:S, :], E), ALU.mult))
                prio_bc = prio[0:S, :].unsqueeze(1).to_broadcast([S, GS, E])
                for top, hot in ((m1, oh1), (m2, oh2)):
                    link(vec.tensor_reduce(top[0:S, :], pr[0:S, :, :], AX, ALU.max))
                    link(vec.tensor_tensor(t7[0:S, :, :], pr[0:S, :, :], bc(top[0:S, :], E), ALU.is_equal))
                    link(vec.tensor_tensor(t7[0:S, :, :], t7[0:S, :, :], prio_bc, ALU.mult))
                    link(vec.tensor_reduce(r1[0:S, :], t7[0:S, :, :], AX, ALU.max))
                    link(vec.tensor_tensor(hot[0:S, :, :], prio_bc, bc(r1[0:S, :], E), ALU.is_equal))
                    if hot is oh1:
                        link(vec.scalar_tensor_tensor(pr[0:S, :, :], oh1[0:S, :, :], -2.0, pr[0:S, :, :],
                                                      ALU.mult, ALU.add))
                vec.tensor_tensor(pick[0:S, :, :], oh1[0:S, :, :], oh2[0:S, :, :], ALU.add).then_inc(pick_ready, 1)
                link(vec.tensor_tensor(r1[0:S, :], m1[0:S, :], m2[0:S, :], ALU.add))
                link(vec.tensor_scalar(r1[0:S, :], r1[0:S, :], 1e-9, None, ALU.add))
                link(vec.reciprocal(r1[0:S, :], r1[0:S, :]))
                vec.wait_ge(meta_stored, at(g, 16 * 2 * GS, 0))
                meta_f = meta[0:S, :, :, :].bitcast(F32)
                for k, top in enumerate((m1, m2)):
                    vec.tensor_tensor(meta_f[:, :, k, 1], top[0:S, :], r1[0:S, :], ALU.mult)
                    last = vec.tensor_copy(meta[0:S, :, k, 0], tokid[0:S, :])
                link(last)
                link(vec.tensor_scalar(tokid[0:S, :], tokid[0:S, :], float(GT), None, ALU.add))

            def places(g):
                vec.wait_ge(A_full[0], at(g, A_USES[0], A0_RANK + 1))
                rank = psA[0][0:S, 0:GS * E].rearrange("p (s e) -> p s e", e=E)
                for s in range(GS):
                    link(vec.tensor_tensor(run[0:S, s + 1, :], run[0:S, s, :],
                                           psA[0][0:S, 64 + s * E:64 + (s + 1) * E], ALU.add))
                vec.tensor_tensor(t7[0:S, :, :], rank, run[0:S, 0:GS, :], ALU.add).then_inc(A_free[0], 1)
                vec.wait_ge(A_free[0], at(g, A_USES[0], A0_RANK + 1))
                for k, hot in enumerate((oh1, oh2)):
                    link(vec.tensor_tensor(hot[0:S, :, :], hot[0:S, :, :], t7[0:S, :, :], ALU.mult))
                    link(vec.tensor_reduce(posf[0:S, :, k], hot[0:S, :, :], AX, ALU.add))
                vec.tensor_copy(pos[0:S, :, :], posf[0:S, :, :]).then_inc(meta_ready, 1)
                link(vec.tensor_copy(run[0:S, 0, :], run[0:S, GS, :]))

            def ffn_piece(g, c):
                if c < HC:
                    vec.wait_ge(G_free[c % 2], at(g, G_USES[c % 2], c // 2 + 1))
                    vec.wait_ge(U_full[c % 2], at(g, U_USES, c // 2 + 1))
                    vec.tensor_tensor(sil[:, c % 2, 0:GT], psU[c % 2][:, 0:GT], sil[:, c % 2, 0:GT], ALU.mult
                                      ).then_inc(hf_ready, 1)
                if c >= 1:
                    vec.wait_ge(hid_hi, at(g, HC, c))
                    vec.tensor_tensor(hid[:, 1, c - 1, 0:GT], sil[:, (c - 1) % 2, 0:GT], hid[:, 0, c - 1, 0:GT],
                                      ALU.subtract).then_inc(hid_lo, 1)

            def ffn_out(g, s):
                vec.wait_ge(hres_ready, at(g, 1, 1))
                if s == 0:
                    vec.wait_ge(out_stored, at(g, 16, 0))
                if s % 2 == 0:
                    vec.wait_ge(Y_full, at(g, Y_USES, s // 2 + 1))
                    src, free = psY, Y_free
                else:
                    vec.wait_ge(G_full[0], at(g, G_USES[0], HC // 2 + s // 2 + 1))
                    src, free = psG[0], G_free[0]
                vec.tensor_tensor(yout[0:S, s, :], src[0:S, 0:D], hres[0:S, s, :], ALU.add).then_inc(free, 1)

            def group(g, first):
                state.update(g=g, n=0)
                ffn = (lambda c: None) if first else (lambda c: ffn_piece(g - 1, c))
                down = (lambda s: None) if first else (lambda s: ffn_out(g - 1, s))
                vec.wait_ge(x_loaded, at(g, 16, 16))
                ffn(0)
                norm(xin, xin, xhat_ready)
                ffn(1)
                split_low(g, 0, first)
                ffn(2)
                ffn(3)
                split_low(g, 1, first)
                ffn(4)
                project_bias(g)
                ffn(5)
                vec.wait_ge(h_ready, at(g, 1, 1))
                norm(h, xn, xn_ready)
                ffn(6)
                split_low(g, 2, first)
                ffn(7)
                values(g)
                ffn(8)
                score_max(g)
                down(0)
                down(1)
                probs_T(g)
                attended(g)
                norm(h2, xn, xn2_ready)
                down(2)
                down(3)
                token_rows_low(g)
                ffn_inputs_low(g)
                top2(g)
                places(g)
                assert state["n"] == STEPS, state["n"]

            group(0, True)
            group(1, False)
            with vec.Fori(2, NG) as g:
                group(g, False)

            state.update(g=NG, n=0)
            link(vec.tensor_tensor(tcount[:, :], run[0:1, 0, :], base_e[0:1, :], ALU.subtract))
            link(vec.tensor_scalar(tcount[:, :], tcount[:, :], float(TILE - 1), None, ALU.add))
            link(vec.tensor_copy(ntile[:, :], tcount[:, :]))
            link(vec.tensor_scalar(ntile[:, :], ntile[:, :], 8, None, ALU.logical_shift_right))
            link(vec.tensor_copy(tcount[:, :], ntile[:, :]))
            link(vec.tensor_copy(tends[:, 0:1], tcount[:, 0:1]))
            for e in range(1, E):
                link(vec.tensor_tensor(tends[:, e:e + 1], tends[:, e - 1:e], tcount[:, e:e + 1], ALU.add))
            vec.tensor_copy(ends_i[:, 0:E], tends[:, :])
            link(vec.tensor_tensor(passed[:, :, :], tile_no[0:1, :].unsqueeze(2).to_broadcast([1, NT, E]),
                                   tends[:, :].unsqueeze(1).to_broadcast([1, NT, E]), ALU.is_ge))
            link(vec.tensor_reduce(ej[:, :], passed[:, :, 0:E - 1], AX, ALU.add))
            link(vec.tensor_tensor(passed[:, :, :], passed[:, :, :],
                                   tcount[:, :].unsqueeze(1).to_broadcast([1, NT, E]), ALU.mult))
            link(vec.tensor_reduce(sj[:, :], passed[:, :, 0:E - 1], AX, ALU.add))
            link(vec.tensor_tensor(sj[:, :], tile_no[0:1, :], sj[:, :], ALU.subtract))
            link(vec.scalar_tensor_tensor(sj[:, :], ej[:, :], float(REGION // TILE), sj[:, :], ALU.mult, ALU.add))
            vec.tensor_copy(plan[:, 2, :], sj[:, :])
            link(vec.tensor_scalar(ej[:, :], ej[:, :], 1.0, None, ALU.add))
            vec.tensor_scalar(plan[:, 1, :], ej[:, :], 16.0, None, ALU.mult)
            for n in range(NS, NE, NS):
                link(vec.tensor_scalar(tj[:, :], ej[:, :], float(NS), float(-NS), ALU.is_ge, ALU.mult))
                link(vec.tensor_tensor(ej[:, :], ej[:, :], tj[:, :], ALU.add))
            vec.tensor_scalar(plan[:, 0, :], ej[:, :], float(SLOT), None, ALU.mult).then_inc(plan_ready, 1)

            for c in range(HC + 1):
                ffn_piece(NG - 1, c)
            for s in range(GS):
                ffn_out(NG - 1, s)

            def tile_T(j, b):
                vec.wait_ge(T_full, at(j, 1, 1) + NG * T_USES)
                vec.tensor_copy(gxT[:, b, :, :, :].rearrange("p a k t -> p (a k t)"), psT_b).then_inc(T_free, 1)

            def tile_piece(j, b, q):
                Q = HC // 2
                if q < Q:
                    vec.wait_ge(G_free[q % 2], at(j, Q // 2, q // 2 + 1) + NG * G_USES[q % 2])
                    vec.wait_ge(U_full[q % 2], at(j, Q // 2, q // 2 + 1) + NG * U_USES)
                    vec.tensor_tensor(sil[:, q % 2, :], psU[q % 2][:, :], sil[:, q % 2, :], ALU.mult
                                      ).then_inc(hf_ready, 1)
                if q >= 1:
                    vec.wait_ge(hid_hi, at(j, Q, q) + NG * HC)
                    vec.tensor_tensor(hidr[:, b, 1, 2 * q - 2:2 * q, :],
                                      sil[:, (q - 1) % 2, :].rearrange("p (c t) -> p c t", c=2),
                                      hidr[:, b, 0, 2 * q - 2:2 * q, :], ALU.subtract).then_inc(hid_lo, 1)

            def tile_out(j, b, k):
                vec.wait_ge(Y_full, at(j, SUB, k + 1) + NG * Y_USES)
                vec.wait_ge(smeta_ready, at(j, 1, 1))
                vec.tensor_scalar(ysb[:, b, k, :], psY[:, 0:D], smeta[:, b, k, 1:2].bitcast(F32), None, ALU.mult
                                  ).then_inc(Y_free, 1)

            def routed_tile(j, b, older, newer):
                tile_piece(j, b, 0)
                tile_piece(j, b, 1)
                if older:
                    tile_out(j - 1, 1 - b, 0)
                tile_piece(j, b, 2)
                if newer:
                    tile_T(j + 1, 1 - b)
                tile_piece(j, b, 3)
                tile_piece(j, b, 4)
                if older:
                    tile_out(j - 1, 1 - b, 1)

            tile_T(0, 0)
            routed_tile(0, 0, False, True)
            routed_tile(1, 1, True, True)
            with vec.Fori(1, NT // 2 - 1) as i:
                for b in range(2):
                    routed_tile(i * 2 + b, b, True, True)
            routed_tile(NT - 2, 0, True, True)
            routed_tile(NT - 1, 1, True, False)
            for k in range(SUB):
                tile_out(NT - 1, 1, k)

        @block.tensor
        def _(pe):
            pe.wait_ge(masks_made, 6)
            pe.wait_ge(consts_loaded, 48)

            def transposes(g, use, src, width):
                pe.wait_ge(T_free, at(g, T_USES, use))
                for s in range(GS):
                    last = pe.transpose(psT[0:width, s * S:(s + 1) * S], src(s), ident[0:S, 0:S])
                last.then_inc(T_full, 1)

            def project(g):
                pe.wait_ge(T_free, at(g, T_USES, T_X + FC))
                for a in range(2):
                    pe.wait_ge(A_free[a], at(g, A_USES[a], A_TOK))
                    for i in range(2):
                        s = 2 * a + i
                        for k in range(FC):
                            last = pe.matmul(psA[a][0:S, i * D:(i + 1) * D], yT[:, k, s * S:(s + 1) * S],
                                             wtok[:, k, :], start=(k == 0), stop=(k == FC - 1))
                    last.then_inc(A_full[a], 1)

            def queries_keys(g, w):
                if w == 0:
                    pe.wait_ge(T_free, at(g, T_USES, T_XN + DC))
                for m in range(DC):
                    pe.wait_ge(A_free[m], at(g, A_USES[m], A_Q + w))
                    for k in range(DC):
                        last = pe.matmul(psA[m][:, 0:GT], wqkv[:, w, k, m * P:(m + 1) * P], xnT[:, k, :],
                                         start=(k == 0), stop=(k == DC - 1))
                    last.then_inc(A_full[m], 1)

            def values(g):
                for a in range(2):
                    pe.wait_ge(A_free[a], at(g, A_USES[a], A_V))
                    for i in range(2):
                        s = 2 * a + i
                        for k in range(DC):
                            last = pe.matmul(psA[a][0:S, i * D:(i + 1) * D], xnT[:, k, s * S:(s + 1) * S],
                                             wqkv[:, 2, k, :], start=(k == 0), stop=(k == DC - 1))
                    last.then_inc(A_full[a], 1)

            def scores(g):
                for m in range(DC):
                    pe.wait_ge(A_free[m], at(g, A_USES[m], A_K + 1))
                pe.wait_ge(T_free, at(g, T_USES, T_SC))
                for s in range(GS):
                    for m in range(DC):
                        last = pe.matmul(psT[0:S, s * S:(s + 1) * S], qT[:, m, s * S:(s + 1) * S],
                                         kT[:, m, s * S:(s + 1) * S], start=(m == 0), stop=(m == DC - 1))
                last.then_inc(T_full, 1)

            def probs_T(g):
                pe.wait_ge(T_free, at(g, T_USES, T_SC + 1))
                pe.wait_ge(A_free[0], at(g, A_USES[0], A0_PT))
                for s in range(GS):
                    last = pe.transpose(psA[0][0:S, s * S:(s + 1) * S], prob[0:S, s, :], ident[0:S, 0:S])
                last.then_inc(A_full[0], 1)

            def attend(g):
                pe.wait_ge(A_free[0], at(g, A_USES[0], A0_PT + 1))
                for a, use in ((1, A1_PV), (0, A0_PV)):
                    pe.wait_ge(A_free[a], at(g, A_USES[a], use))
                    for i in range(2):
                        s = 2 * (1 - a) + i
                        last = pe.matmul(psA[a][0:S, i * D:(i + 1) * D], probT[0:S, s, :], v[0:S, s, :],
                                         start=True, stop=True)
                    last.then_inc(A_full[a], 1)

            def router(g):
                pe.wait_ge(T_free, at(g, T_USES, T_X2 + DC))
                for k in range(DC):
                    last = pe.matmul(psT[0:E, 0:GT], wrt[:, k, :], xnT[:, k, :], start=(k == 0),
                                     stop=(k == DC - 1))
                last.then_inc(T_full, 1)

            def logits(g):
                pe.wait_ge(T_free, at(g, T_USES, T_LG + 1))
                wait_apart(pe, A_free[1], at(g, A_USES[1], A1_LG))
                for s in range(GS):
                    last = pe.transpose(psA[1][0:S, s * 8:s * 8 + E], logT[:, s * S:(s + 1) * S], ident[0:E, 0:E])
                last.then_inc(A_full[1], 1)

            def ranks(g):
                pe.wait_ge(pick_ready, at(g, 1, 1))
                pe.wait_ge(A_free[0], at(g, A_USES[0], A0_RANK))
                picks = pick[0:S, :, :].rearrange("p s e -> p (s e)")
                pe.matmul(psA[0][0:S, 0:GS * E], before[0:S, 0:S], picks, start=True, stop=True)
                pe.matmul(psA[0][0:S, 64:64 + GS * E], ones_b[0:S, 0:S], picks, start=True, stop=True
                          ).then_inc(A_full[0], 1)

            def ffn_piece(g, c):
                if c == 0:
                    pe.wait_ge(x2_hi, at(g, DC, DC))
                    pe.wait_ge(x2_lo, at(g, DC, DC))
                for which, ps, full in ((0, psG, G_full), (1, psU, U_full)):
                    if which == 0:
                        pe.wait_ge(G_free[c % 2], at(g, G_USES[c % 2], c // 2))
                    else:
                        pe.wait_ge(hf_ready, at(g, HC, max(c - 1, 0)))
                    n = 0
                    for wp, xp in TERMS:
                        for k in range(DC):
                            last = pe.matmul(ps[c % 2][:, 0:GT], wcols(0, which, wp, k * DFF + c * P, P),
                                             x2T[:, xp, k, :], start=(n == 0), stop=(n == 3 * DC - 1))
                            n += 1
                    last.then_inc(full[c % 2], 1)

            def ffn_down(g, s):
                if s == 0:
                    pe.wait_ge(hid_hi, at(g, HC, HC))
                    pe.wait_ge(hid_lo, at(g, HC, HC))
                if s % 2 == 0:
                    pe.wait_ge(Y_free, at(g, Y_USES, s // 2))
                    dst, full = psY, Y_full
                else:
                    pe.wait_ge(G_free[0], at(g, G_USES[0], HC // 2 + s // 2))
                    dst, full = psG[0], G_full[0]
                n = 0
                for wp, xp in TERMS:
                    for c in range(HC):
                        last = pe.matmul(dst[0:S, 0:D], hid[:, xp, c, s * S:(s + 1) * S],
                                         wcols(0, 2, wp, c * D, D), start=(n == 0), stop=(n == 3 * HC - 1))
                        n += 1
                last.then_inc(full, 1)

            def group(g, first):
                ffn = (lambda c: None) if first else (lambda c: ffn_piece(g - 1, c))
                down = (lambda s: None) if first else (lambda s: ffn_down(g - 1, s))
                ffn(0)
                ffn(1)
                pe.wait_ge(xhat_ready, at(g, 1, 1))
                for k in range(FC):
                    transposes(g, T_X + k, lambda s: xin[0:S, s, k * P:(k + 1) * P], P)
                    if k % 2 == 1:
                        ffn(2 + k // 2)
                project(g)
                ffn(4)
                ffn(5)
                pe.wait_ge(xn_ready, at(g, 1, 1))
                transposes(g, T_XN, lambda s: xn[0:S, s, 0:P], P)
                ffn(6)
                transposes(g, T_XN + 1, lambda s: xn[0:S, s, P:2 * P], P)
                queries_keys(g, 0)
                queries_keys(g, 1)
                ffn(7)
                values(g)
                scores(g)
                down(0)
                down(1)
                probs_T(g)
                attend(g)
                down(2)
                down(3)
                pe.wait_ge(xn2_ready, at(g, 1, 1))
                transposes(g, T_X2, lambda s: xn[0:S, s, 0:P], P)
                transposes(g, T_X2 + 1, lambda s: xn[0:S, s, P:2 * P], P)
                router(g)
                logits(g)
                ranks(g)

            group(0, True)
            pe.wait_ge(split_lo, 3)
            group(1, False)
            with pe.Fori(2, NG) as g:
                group(g, False)
            for c in range(HC):
                ffn_piece(NG - 1, c)
            for s in range(GS):
                ffn_down(NG - 1, s)

            pe.wait_ge(plan_ready, 1)

            def tile_T(j, b):
                pe.wait_ge(grow_loaded, at(j, 16 * SUB, 16 * SUB))
                pe.wait_ge(T_free, at(j, 1, 0) + NG * T_USES)
                for a in range(2):
                    for k in range(DC):
                        for r in range(SUB):
                            last = pe.transpose(psT_b[:, ((a * DC + k) * SUB + r) * P:((a * DC + k) * SUB + r + 1) * P],
                                                grow[:, b, r, (a * DC + k) * P:(a * DC + k + 1) * P], ident_b[:, :])
                last.then_inc(T_full, 1)

            def tile_piece(j, b, q, slot_at):
                Q = HC // 2
                if q == 0:
                    pe.wait_ge(T_free, at(j, 1, 1) + NG * T_USES)
                for which, ps, full in ((0, psG, G_full), (1, psU, U_full)):
                    if which == 0:
                        pe.wait_ge(G_free[q % 2], at(j, Q // 2, q // 2) + NG * G_USES[q % 2])
                    else:
                        pe.wait_ge(hf_ready, at(j, Q, max(q - 1, 0)) + NG * HC)
                    for i in range(2):
                        c = 2 * q + i
                        n = 0
                        for wp, xp in TERMS:
                            for k in range(DC):
                                last = pe.matmul(ps[q % 2][:, i * TILE:(i + 1) * TILE],
                                                 wcols(slot_at, which, wp, k * DFF + c * P, P),
                                                 gxT[:, b, xp, k, :], start=(n == 0), stop=(n == 3 * DC - 1))
                                n += 1
                    last.then_inc(full[q % 2], 1)

            def tile_down(j, b, r, slot_at):
                if r == 0:
                    pe.wait_ge(hid_hi, at(j, HC // 2, HC // 2) + NG * HC)
                    pe.wait_ge(hid_lo, at(j, HC // 2, HC // 2) + NG * HC)
                pe.wait_ge(Y_free, at(j, SUB, r) + NG * Y_USES)
                n = 0
                for wp, xp in TERMS:
                    for c in range(HC):
                        last = pe.matmul(psY[:, 0:D], hidr[:, b, xp, c, r * P:(r + 1) * P],
                                         wcols(slot_at, 2, wp, c * D, D), start=(n == 0), stop=(n == 3 * HC - 1))
                        n += 1
                last.then_inc(Y_full, 1)

            def slot_of(j):
                return pe.value_load(plan[0:1, 0, bass.ds(j, 1)], min_val=0, max_val=(NS - 1) * SLOT)

            def routed_tile(j, b, older, newer):
                loads = pe.value_load(plan[0:1, 1, bass.ds(j, 1)], min_val=16, max_val=16 * E)
                here = slot_of(j)
                pe.wait_ge(expert_loaded, loads)
                tile_piece(j, b, 0, here)
                tile_piece(j, b, 1, here)
                if older:
                    tile_down(j - 1, 1 - b, 0, slot_of(j - 1))
                tile_piece(j, b, 2, here)
                if newer:
                    tile_T(j + 1, 1 - b)
                tile_piece(j, b, 3, here)
                if older:
                    tile_down(j - 1, 1 - b, 1, slot_of(j - 1))

            tile_T(0, 0)
            routed_tile(0, 0, False, True)
            routed_tile(1, 1, True, True)
            with pe.Fori(1, NT // 2 - 1) as i:
                for b in range(2):
                    routed_tile(i * 2 + b, b, True, True)
            routed_tile(NT - 2, 0, True, True)
            routed_tile(NT - 1, 1, True, False)
            for r in range(SUB):
                tile_down(NT - 1, 1, r, slot_of(NT - 1))


def kernel(**inputs):
    import numpy as np
    import concourse.bacc as bacc
    from concourse.bass_utils import run_bass_kernel_spmd

    a = {k: np.asarray(t) for k, t in inputs.items()}

    def ffn_layout(gate, up, down):
        return np.stack([w.T.reshape(-1, P, w.shape[0]).transpose(1, 0, 2).reshape(P, -1)
                         for w in (gate, up, down)])

    ffn = [ffn_layout(a["L0_ffn_shared_gate"], a["L0_ffn_shared_up"], a["L0_ffn_shared_down"])]
    for e in range(E):
        ffn.append(ffn_layout(a["L0_ffn_routed_gate"][e], a["L0_ffn_routed_up"][e], a["L0_ffn_routed_down"][e]))
    arrays = {
        "in_x": a["x"].reshape(B, S, FAN),
        "in_columns": np.concatenate([a[k].reshape(-1, P).T for k in (
            "L0_tok_ln_gamma", "L0_tok_ln_beta", "L0_attn_b_q", "L0_attn_b_k")], axis=1),
        "in_w_tok": np.ascontiguousarray(a["L0_tok_W"].T),
        "in_b_tok": a["L0_tok_b"],
        "in_w_qkv": np.stack([a["L0_attn_W_q"], a["L0_attn_W_k"], a["L0_attn_W_v"]]),
        "in_b_v": a["L0_attn_b_v"],
        "in_w_ffn": np.stack(ffn),
        "in_w_router": np.ascontiguousarray(a["L0_ffn_router_w"].T),
    }
    nc = bacc.Bacc("TRN2", target_bir_lowering=False, num_devices=1)
    args = [nc.dram_tensor(n, t.shape, mybir.dt.from_np(t.dtype), kind="ExternalInput").ap()
            for n, t in arrays.items()]
    out = nc.dram_tensor("out", (NTOK + TILE, D), F32, kind="ExternalOutput").ap()
    audio_tower(nc, *args, out)
    r = run_bass_kernel_spmd(nc, [arrays], core_ids=[0])
    return r.results[0]["out"][:NTOK].reshape(B, S, D)
```

```python
from contextlib import ExitStack

import concourse.bass as bass
from concourse import mybir

F32 = mybir.dt.float32
BF16 = mybir.dt.bfloat16
I32 = mybir.dt.int32
ALU = mybir.AluOpType
ACT = mybir.ActivationFunctionType
AX = mybir.AxisListType.X

P = 128
B, T_IN, C = 32, 250, 256
FAN = 2 * C
S = T_IN // 2
NTOK = B * S
D = 256
DC = D // P
FC = FAN // P
DFF = 1024
HC = DFF // P
E = 7
NE = E + 1
GS = 4
NG = B // GS
GT = GS * S

TILE = 256
SUB = TILE // P
NT = (2 * NTOK + E * (TILE - 1)) // TILE
REGION = 4096
TABLE = (E - 1) * REGION + NT * TILE
NS = 3
PART = 2048
SLOT = 3 * 2 * PART
EPS = 1e-5
RSQRT_SEED = float(0x5F3759DF)

assert NT % 2 == 0 and NTOK <= REGION and TABLE % P == 0 and NG == E + 1


def audio_tower(nc, x, columns, w_tok, b_tok, w_qkv, b_v, w_ffn, w_router, out):
    with ExitStack() as ctx:
        def sb(name, shape, dt=F32):
            return ctx.enter_context(nc.sbuf_tensor(name, shape, dt))

        def bank(name):
            return ctx.enter_context(nc.psum_tensor(name, [P, 512], F32))

        def sem(name):
            return ctx.enter_context(nc.semaphore(name))

        token_rows = nc.dram_tensor("token_rows", [NTOK, 2 * D], BF16).ap()
        choices = nc.dram_tensor("choices", [TABLE, 2], I32).ap()
        split_ffn = nc.dram_tensor("split_ffn", [E, 3, P, 2 * PART], BF16).ap()

        ident = sb("ident", [P, P])
        ident_b = sb("ident_b", [P, P], BF16)
        before = sb("before", [P, P], BF16)
        ones_b = sb("ones_b", [P, P], BF16)
        wtok = sb("wtok", [P, FC, D])
        wqkv = sb("wqkv", [P, 3, DC, D])
        wrt = sb("wrt", [P, DC, E])
        cols = sb("cols", [P, 2 * FC + 2 * DC])
        gam, bet = cols[:, 0:FC], cols[:, FC:2 * FC]
        bqk = cols[:, 2 * FC:].rearrange("p (w c) -> p w c", w=2)
        btok2 = sb("btok2", [P, 2, D])
        bv2 = sb("bv2", [P, 2, D])
        prio = sb("prio", [P, E])
        base_e = sb("base_e", [P, E])
        tokid = sb("tokid", [P, GS])
        iota_i = sb("iota_i", [P, 64], I32)
        tile_no = sb("tile_no", [P, NT])

        xin = sb("xin", [P, GS, FAN])
        yT = sb("yT", [P, FC, GT])
        hpre = sb("hpre", [P, GS, D])
        h = sb("h", [P, GS, D])
        xn = sb("xn", [P, GS, D])
        xnT = sb("xnT", [P, DC, GT])
        qT = sb("qT", [P, DC, GT])
        kT = sb("kT", [P, DC, GT])
        v = sb("v", [P, GS, D])
        prob = sb("prob", [P, GS, S])
        probT = sb("probT", [P, GS, S])
        h2 = hpre
        stats = sb("stats", [P, GS, 6])
        mv = sb("mv", [P, GS, 2])
        ve = sb("ve", [P, GS])
        hv = sb("hv", [P, GS])
        rs = sb("rs", [P, GS])
        sq = sb("sq", [P, GS])
        smax = sb("smax", [P, GS])
        ssum = sb("ssum", [P, GS])
        logT = sb("logT", [E, GT])
        lg = sb("lg", [P, GS, E])
        pr = sb("pr", [P, GS, E])
        t7 = sb("t7", [P, GS, E])
        oh1 = sb("oh1", [P, GS, E])
        oh2 = sb("oh2", [P, GS, E])
        pick = sb("pick", [P, GS, E], BF16)
        run = sb("run", [P, GS + 1, E])
        m1 = sb("m1", [P, GS])
        m2 = sb("m2", [P, GS])
        r1 = sb("r1", [P, GS])
        posf = sb("posf", [P, GS, 2])
        pos = sb("pos", [P, GS, 2], I32)
        meta = sb("meta", [P, GS, 2, 2], I32)
        rows = sb("rows", [P, GS, 2 * D], BF16)
        x2T = sb("x2T", [P, 2, DC, GT], BF16)
        hres = sb("hres", [P, GS, D])
        yout = sb("yout", [P, GS, D])
        hid = sb("hid", [P, 2, HC, 512], BF16)
        hidr = hid[:].rearrange("p a c (b t) -> p b a c t", b=2)
        sil = sb("sil", [P, 2, 512])
        stage = sb("stage", [P, PART])
        split = sb("split", [P, 2, PART], BF16)
        W = sb("W", [P, NS * SLOT], BF16)
        grow = sb("grow", [P, 2, SUB, 2 * D], BF16)
        gxT = sb("gxT", [P, 2, 2, DC, TILE], BF16)
        gmeta = sb("gmeta", [P, 2, SUB, 2], I32)
        smeta = sb("smeta", [P, 2, SUB, 2], I32)
        gidx = sb("gidx", [P, 2, SUB], I32)
        ysb = sb("ysb", [P, 2, SUB, D])
        ntile = sb("ntile", [1, E], I32)
        tends = sb("tends", [1, E])
        tcount = sb("tcount", [1, E])
        ends_i = sb("ends_i", [1, 8], I32)
        passed = sb("passed", [1, NT, E])
        ej = sb("ej", [1, NT])
        sj = sb("sj", [1, NT])
        tj = sb("tj", [1, NT])
        plan = sb("plan", [1, 3, NT], I32)
        padfill = grow[:].rearrange("p a b c -> p (a b c)").bitcast(I32)[:, 0:TABLE // P * 2].rearrange("p (r w) -> p r w", w=2)

        psT, psA0, psA1, psY = bank("psT"), bank("psA0"), bank("psA1"), bank("psY")
        psG = [bank("psG0"), bank("psG1")]
        psU = [bank("psU0"), bank("psU1")]
        psA = [psA0, psA1]
        psT_b = psT[:, :].bitcast(BF16)

        T_full, T_free = sem("T_full"), sem("T_free")
        A_full, A_free = [sem("A0_full"), sem("A1_full")], [sem("A0_free"), sem("A1_free")]
        Y_full, Y_free = sem("Y_full"), sem("Y_free")
        G_full, G_free = [sem("G0_full"), sem("G1_full")], [sem("G0_free"), sem("G1_free")]
        U_full = [sem("U0_full"), sem("U1_full")]
        T_X0, T_X2, T_XN0, T_SC, T_H0, T_LT, T_USES = range(7)
        A0_X1, A0_TOK, A0_Q, A0_K, A0_V, A0_PT, A0_PV, A0_USES = range(8)
        A1_X3, A1_TOK, A1_XN1, A1_Q, A1_K, A1_V, A1_PV, A1_H1, A1_USES = range(9)
        Y_LG, Y_RANK, Y_D0, Y_D2, Y_USES = range(5)
        G_USES, U_USES = [HC // 2 + 2, HC // 2], HC // 2
        A_USES, A_TOK, A_V, A_PV = (A0_USES, A1_USES), (A0_TOK, A1_TOK), (A0_V, A1_V), (A0_PV, A1_PV)
        A_QK = ((A0_Q, A1_Q), (A0_K, A1_K))
        IN_T, IN_A0, IN_A1 = ((psT, T_full, T_free, T_USES), (psA0, A_full[0], A_free[0], A0_USES),
                              (psA1, A_full[1], A_free[1], A1_USES))
        X_AT = [(*IN_T, T_X0), (*IN_A0, A0_X1), (*IN_T, T_X2), (*IN_A1, A1_X3)]
        XN_AT = [(*IN_T, T_XN0), (*IN_A1, A1_XN1)]
        H_AT = [(*IN_T, T_H0), (*IN_A1, A1_H1)]

        consts_loaded, masks_made, biases_loaded = sem("consts_loaded"), sem("masks_made"), sem("biases_loaded")
        iota_made, indices_made = sem("iota_made"), sem("indices_made")
        pads_masked, pads_made, pads_stored = sem("pads_masked"), sem("pads_made"), sem("pads_stored")
        x_loaded, xhat_ready = sem("x_loaded"), sem("xhat_ready")
        h_ready, xn_ready = sem("h_ready"), sem("xn_ready")
        smax_ready = sem("smax_ready")
        hres_ready, xn2_ready = sem("hres_ready"), sem("xn2_ready")
        rows_hi, rows_lo, rows_stored = sem("rows_hi"), sem("rows_lo"), sem("rows_stored")
        x2_f32, x2_hi, x2_lo = sem("x2_f32"), sem("x2_hi"), sem("x2_lo")
        e_ready = sem("e_ready")
        pick_ready, meta_ready, meta_stored = sem("pick_ready"), sem("meta_ready"), sem("meta_stored")
        dve_step, x_step, route_step = sem("dve_step"), sem("x_step"), sem("route_step")
        plan_step, passed_by = sem("plan_step"), sem("passed_by")
        sil_ready, hf_ready, hid_hi, hid_lo = sem("sil_ready"), sem("hf_ready"), sem("hid_hi"), sem("hid_lo")
        out_stored = sem("out_stored")
        stage_loaded, split_hi, split_lo, split_stored = (
            sem("stage_loaded"), sem("split_hi"), sem("split_lo"), sem("split_stored"))
        plan_ready, expert_loaded = sem("plan_ready"), sem("expert_loaded")
        gmeta_loaded, gidx_ready, grow_loaded = sem("gmeta_loaded"), sem("gidx_ready"), sem("grow_loaded")
        smeta_ready, added = sem("smeta_ready"), sem("added")

        def at(g, per_group, n):
            return g * per_group + n

        def wait_apart(eng, sem, value):
            eng.wait_ge(sem, value).then_inc(passed_by, 1)

        def wcols(slot_at, which, part, first, n):
            return W[:, bass.ds(slot_at + (2 * which + part) * PART + first, n)]

        TERMS = ((0, 0), (0, 1), (1, 0))
        x_groups = x.rearrange("(g s) p f -> g p s f", s=GS)
        out_groups = out[0:NTOK, :].rearrange("(g s p) d -> g p s d", s=GS, p=S)
        rows_groups = token_rows.rearrange("(g s p) d -> g p s d", s=GS, p=S)
        w_stage = w_ffn.rearrange("e t p n -> (e t) p n")
        split_steps = split_ffn.rearrange("e t p n -> (e t) p n")
        choice_tiles = choices.rearrange("(r p k) w -> r p (k w)", p=P, k=SUB)

        block = ctx.enter_context(nc.Block())

        @block.sync
        def _(sp):
            def load_stage(step):
                sp.dma_start(stage[:, :], w_stage[step, :, :]).then_inc(stage_loaded, 16)

            def load_x(g):
                sp.dma_start(xin[0:S, :, :], x_groups[g, :, :, :]).then_inc(x_loaded, 16)

            def split_traffic(g, first):
                for t in range(3):
                    sp.wait_ge(split_lo, at(g, 3, t + 1))
                    load_stage(g * 3 + t + 1)
                    if not first:
                        sp.dma_start(split_steps[(g - 1) * 3 + t, :, :],
                                     split[:, :, :].rearrange("p a n -> p (a n)")).then_inc(split_stored, 16)

            load_x(0)
            load_stage(0)
            sp.dma_start(wtok[:, :, :], w_tok.rearrange("(c p) n -> p c n", p=P)).then_inc(consts_loaded, 16)
            sp.dma_start(wqkv[:, :, :, :], w_qkv.rearrange("w (c p) n -> p w c n", p=P)).then_inc(consts_loaded, 16)
            sp.dma_start(wrt[:, :, :], w_router.rearrange("(c p) n -> p c n", p=P)).then_inc(consts_loaded, 16)

            def rest_of_group(g, first):
                sp.wait_ge(A_full[1], at(g, A1_USES, A1_X3 + 1))
                load_x(g + 1)
                split_traffic(g, first)
                sp.wait_ge(rows_hi, at(g, 1, 1))
                sp.wait_ge(rows_lo, at(g, 1, 1))
                sp.dma_start(rows_groups[g, :, :, :], rows[0:S, :, :]).then_inc(rows_stored, 16)

            def store_out(g):
                sp.wait_ge(Y_free, at(g, Y_USES, Y_USES))
                sp.wait_ge(G_free[0], at(g, G_USES[0], G_USES[0]))
                sp.dma_start(out_groups[g, :, :, :], yout[0:S, :, :]).then_inc(out_stored, 16)

            rest_of_group(0, True)
            rest_of_group(1, False)
            store_out(0)
            with sp.Fori(2, NG - 1) as g:
                rest_of_group(g, False)
                store_out(g - 1)
            for t in range(3):
                sp.wait_ge(split_lo, (NG - 1) * 3 + t + 1)
                if t < 2:
                    load_stage((NG - 1) * 3 + t + 1)
                sp.dma_start(split_steps[(NG - 2) * 3 + t, :, :],
                             split[:, :, :].rearrange("p a n -> p (a n)")).then_inc(split_stored, 16)
            sp.wait_ge(rows_hi, NG)
            sp.wait_ge(rows_lo, NG)
            sp.dma_start(rows_groups[NG - 1, :, :, :], rows[0:S, :, :]).then_inc(rows_stored, 16)
            store_out(NG - 2)

            sp.wait_ge(split_stored, 16 * 3 * E)
            for n in range(1, NE):
                if n == NS:
                    store_out(NG - 1)
                if n == NS + 1:
                    sp.wait_ge(plan_ready, 1)
                if n > NS:
                    ended = sp.value_load(ends_i[0:1, n - NS - 1:n - NS], min_val=0, max_val=NT)
                    sp.wait_ge(Y_full, ended * SUB + NG * Y_USES)
                sp.dma_start(
                    W[:, (n % NS) * SLOT:(n % NS + 1) * SLOT].rearrange("p (t n) -> p t n", t=3),
                    split_ffn[n - 1, :, :, :].rearrange("t p n -> p t n")).then_inc(expert_loaded, 16)
                sp.wait_ge(expert_loaded, 16 * n)
            sp.wait_ge(out_stored, 16 * NG)
            sp.wait_ge(added, 16 * SUB * NT)

        @block.gpsimd
        def _(pool):
            def iota(dst, pattern, base, mult):
                pool.iota(dst, pattern, base=base, channel_multiplier=mult).then_inc(iota_made, 1)

            pool.memset(ident[:, :], 0.0).then_inc(masks_made, 1)
            pool.memset(before[:, :], 1.0).then_inc(masks_made, 1)
            pool.memset(ones_b[:, :], 1.0).then_inc(masks_made, 1)
            pool.memset(yout[:, 0:2, :], 0.0).then_inc(pads_made, 1)
            pool.memset(padfill[:, :, 1], 0).then_inc(pads_made, 1)
            iota(padfill[:, :, 0], [[1, TABLE // P]], 0, TABLE // P)
            iota(iota_i[:, 0:E], [[-1, E]], E, 0)
            iota(iota_i[:, 8:8 + E], [[REGION, E]], 0, 0)
            iota(iota_i[:, 16:16 + GS], [[S, GS]], 0, 1)
            iota(iota_i[:, 20:20 + NT], [[1, NT]], 0, 0)
            pool.wait_ge(pads_made, 3)
            pool.dma_start(choices.rearrange("(p r) w -> p r w", p=P), padfill).then_inc(pads_stored, 16)
            pool.dma_start(out[NTOK:NTOK + TILE, :].rearrange("(k p) d -> p k d", p=P), yout[:, 0:2, :]
                           ).then_inc(pads_stored, 16)
            pool.wait_ge(masks_made, 3)
            pool.affine_select(out=ident[:, :], in_=ident[:, :], compare_op=ALU.not_equal, fill=1.0, base=0,
                               pattern=[[-1, P]], channel_multiplier=1).then_inc(masks_made, 1)
            pool.affine_select(out=before[:, :], in_=before[:, :], compare_op=ALU.is_gt, fill=0.0, base=0,
                               pattern=[[1, P]], channel_multiplier=-1).then_inc(masks_made, 1)
            pool.wait_ge(masks_made, 5)
            pool.tensor_copy(ident_b[:, :], ident[:, :]).then_inc(masks_made, 1)
            pool.wait_ge(pads_stored, 32)

            def residual(g, first):
                wait_apart(pool, A_free[0], at(g, A0_USES, A0_PV + 1))
                if not first:
                    wait_apart(pool, G_free[0], at(g - 1, G_USES[0], G_USES[0]))
                pool.tensor_copy(hres[0:S, :, :], h2[0:S, :, :]).then_inc(hres_ready, 1)

            def store_choices(g):
                wait_apart(pool, meta_ready, at(g, 1, 1))
                for s in range(GS):
                    for k in range(2):
                        pool.indirect_dma_start(
                            choices[:, :], bass.IndirectOffsetOnAxis(ap=pos[0:S, s, k:k + 1], axis=0),
                            meta[0:S, s, k, :], None).then_inc(meta_stored, 16)

            residual(0, True)
            store_choices(0)
            residual(1, False)
            store_choices(1)
            with pool.Fori(2, NG) as g:
                residual(g, False)
                store_choices(g)

            pool.wait_ge(plan_ready, 1)
            pool.wait_ge(meta_stored, 16 * 2 * GS * NG)
            pool.wait_ge(rows_stored, 16 * NG)

            def load_choices(j, b):
                row = pool.value_load(plan[0:1, 2, bass.ds(j, 1)], min_val=0, max_val=TABLE // TILE - 1)
                pool.dma_start(gmeta[:, b, :, :].rearrange("p k w -> p (k w)"),
                               choice_tiles[bass.ds(row, 1), :, :].rearrange("r p n -> (r p) n")
                               ).then_inc(gmeta_loaded, 16)
                wait_apart(pool, gmeta_loaded, at(j, 16, 16))
                pool.tensor_scalar(gidx[:, b, :], gmeta[:, b, :, 0], NTOK - 1, None, ALU.min).then_inc(gidx_ready, 1)
                wait_apart(pool, gidx_ready, at(j, 1, 1))

            def gather_rows(j, b):
                for k in range(SUB):
                    pool.indirect_dma_start(
                        grow[:, b, k, :], None, token_rows[:, :],
                        bass.IndirectOffsetOnAxis(ap=gidx[:, b, k:k + 1], axis=0)).then_inc(grow_loaded, 16)

            def keep_meta(j, b):
                pool.tensor_copy(smeta[:, b, :, :], gmeta[:, b, :, :]).then_inc(smeta_ready, 1)

            def add_rows(j, b):
                wait_apart(pool, Y_free, at(j, SUB, SUB) + NG * Y_USES)
                for k in range(SUB):
                    pool.indirect_dma_start(
                        out[:, :], bass.IndirectOffsetOnAxis(ap=smeta[:, b, k, 0:1], axis=0),
                        ysb[:, b, k, :], None, compute_op=ALU.add).then_inc(added, 16)

            def tile_steps(j, b, older, newer):
                if older >= 2:
                    wait_apart(pool, added, at(j - 1, 16 * SUB, 0))
                keep_meta(j, b)
                if newer:
                    pool.wait_ge(smeta_ready, at(j, 1, 1))
                    load_choices(j + 2, b)
                    wait_apart(pool, T_full, at(j, 1, 1) + NG * T_USES)
                    gather_rows(j + 2, b)
                if older >= 1:
                    add_rows(j - 1, 1 - b)

            for b in range(2):
                load_choices(b, b)
                gather_rows(b, b)
                pool.wait_ge(grow_loaded, 16 * SUB * (b + 1))
            tile_steps(0, 0, 0, True)
            pool.wait_ge(out_stored, 16 * NG)
            tile_steps(1, 1, 1, True)
            with pool.Fori(1, NT // 2 - 1) as i:
                for b in range(2):
                    tile_steps(i * 2 + b, b, 2, True)
            for b in range(2):
                tile_steps(NT - 2 + b, b, 2, False)
            pool.wait_ge(added, 16 * SUB * (NT - 1))
            add_rows(NT - 1, 1)
            pool.wait_ge(added, 16 * SUB * NT)

        @block.scalar
        def _(act):
            act.dma_start(cols[:, :], columns).then_inc(biases_loaded, 16)
            for s in range(2):
                act.dma_start(btok2[:, s, :], b_tok.partition_broadcast(P)).then_inc(biases_loaded, 16)
                act.dma_start(bv2[:, s, :], b_v.partition_broadcast(P)).then_inc(biases_loaded, 16)
            act.wait_ge(biases_loaded, 16 * 5)

            def split_high(g, t, first):
                act.wait_ge(stage_loaded, at(g, 48, 16 * (t + 1)))
                if first:
                    dst = W[:, 2 * t * PART:(2 * t + 1) * PART]
                else:
                    act.wait_ge(split_stored, at(g - 1, 48, 16 * t))
                    dst = split[:, 0, :]
                act.activation(dst, stage[:, :], ACT.Copy).then_inc(split_hi, 1)

            def token_inputs(g, k):
                bank_, full, free, uses, use = X_AT[k]
                act.wait_ge(full, at(g, uses, use + 1))
                act.activation(yT[:, k, :], bank_[:, 0:GT], ACT.Identity, bias=bet[:, k:k + 1],
                               scale=gam[:, k:k + 1]).then_inc(free, 1)

            def relu(g, a):
                act.wait_ge(A_free[a], at(g, A_USES[a], A_TOK[a] + 1))
                act.activation(h[0:S, 2 * a:2 * a + 2, :], hpre[0:S, 2 * a:2 * a + 2, :], ACT.Relu
                               ).then_inc(h_ready, 1)

            def normed_T(g, k, where):
                bank_, full, free, uses, use = where[k]
                act.wait_ge(full, at(g, uses, use + 1))
                act.activation(xnT[:, k, :], bank_[:, 0:GT], ACT.Copy).then_inc(free, 1)

            def queries_keys(g, w):
                for m in range(DC):
                    act.wait_ge(A_full[m], at(g, A_USES[m], A_QK[w][m] + 1))
                    act.activation((qT, kT)[w][:, m, :], psA[m][:, 0:GT], ACT.Identity,
                                   bias=bqk[:, w, m:m + 1]).then_inc(A_free[m], 1)

            def exps(g):
                act.wait_ge(smax_ready, at(g, 1, 1))
                for s in range(GS):
                    last = act.activation(prob[0:S, s, :], psT[0:S, s * S:(s + 1) * S], ACT.Exp,
                                          bias=smax[0:S, s:s + 1], scale=D ** -0.5, accum_out=ssum[0:S, s:s + 1])
                last.then_inc(T_free, 1)

            def token_rows_high(g):
                act.wait_ge(xn2_ready, at(g, 1, 1))
                act.wait_ge(rows_stored, at(g, 16, 0))
                act.activation(rows[0:S, :, 0:D], xn[0:S, :, :], ACT.Copy).then_inc(rows_hi, 1)

            def ffn_inputs(g):
                for k in range(DC):
                    normed_T(g, k, H_AT)
                for k in range(DC):
                    bank_, full, free, uses, use = H_AT[k]
                    act.wait_ge(free, at(g, uses, use + 1))
                    act.activation(x2T[:, 0, k, :], xnT[:, k, :], ACT.Copy).then_inc(x2_hi, 1)

            def router_T(g):
                act.wait_ge(T_full, at(g, T_USES, T_LT + 1))
                act.activation(logT[:, :], psT[0:E, 0:GT], ACT.Copy).then_inc(T_free, 1)

            def router_exp(g):
                act.wait_ge(Y_free, at(g, Y_USES, Y_LG + 1))
                act.activation(pr[0:S, :, :], lg[0:S, :, :], ACT.Exp).then_inc(e_ready, 1)

            def ffn_piece(g, c):
                if c < HC:
                    act.wait_ge(G_full[c % 2], at(g, G_USES[c % 2], c // 2 + 1))
                    act.wait_ge(hid_lo, at(g, HC, max(c - 1, 0)))
                    act.activation(sil[:, c % 2, 0:GT], psG[c % 2][:, 0:GT], ACT.Silu).then_inc(G_free[c % 2], 1)
                if c >= 1:
                    act.wait_ge(hf_ready, at(g, HC, c))
                    if c == 1:
                        act.wait_ge(G_free[0], at(g, G_USES[0], 0))
                    act.activation(hid[:, 0, c - 1, 0:GT], sil[:, (c - 1) % 2, 0:GT], ACT.Copy).then_inc(hid_hi, 1)

            def group(g, first=False):
                ffn = (lambda c: None) if first else (lambda c: ffn_piece(g - 1, c))
                if not first:
                    router_exp(g - 1)
                token_inputs(g, 0)
                token_inputs(g, 1)
                ffn(0)
                token_inputs(g, 2)
                token_inputs(g, 3)
                ffn(1)
                split_high(g, 0, first)
                relu(g, 0)
                relu(g, 1)
                for c in range(2, 6):
                    ffn(c)
                normed_T(g, 0, XN_AT)
                normed_T(g, 1, XN_AT)
                ffn(6)
                split_high(g, 1, first)
                queries_keys(g, 0)
                queries_keys(g, 1)
                ffn(7)
                ffn(8)
                exps(g)
                split_high(g, 2, first)
                token_rows_high(g)
                ffn_inputs(g)
                router_T(g)

            group(0, True)
            group(1)
            with act.Fori(2, NG) as g:
                group(g)
            router_exp(NG - 1)
            for c in range(HC + 1):
                ffn_piece(NG - 1, c)

            def routed_tile(j, b, first):
                Q = HC // 2
                for q in range(Q + 1):
                    if q < Q:
                        act.wait_ge(G_full[q % 2], at(j, Q // 2, q // 2 + 1) + NG * G_USES[q % 2])
                        act.wait_ge(hid_lo, at(j, Q, max(q - 1, 0)) + NG * HC)
                        act.activation(sil[:, q % 2, :], psG[q % 2][:, :], ACT.Silu).then_inc(G_free[q % 2], 1)
                    if q >= 1:
                        act.wait_ge(hf_ready, at(j, Q, q) + NG * HC)
                        if q == 1 and first:
                            act.wait_ge(G_free[0], NG * G_USES[0])
                        elif q == 1:
                            act.wait_ge(Y_full, (j - 1) * SUB + NG * Y_USES)
                        act.activation(hidr[:, b, 0, 2 * q - 2:2 * q, :],
                                       sil[:, (q - 1) % 2, :].rearrange("p (c t) -> p c t", c=2),
                                       ACT.Copy).then_inc(hid_hi, 1)

            for b in range(2):
                routed_tile(b, b, True)
            with act.Fori(1, NT // 2) as i:
                for b in range(2):
                    routed_tile(i * 2 + b, b, False)

        @block.vector
        def _(vec):
            vec.wait_ge(iota_made, 5)
            vec.tensor_scalar(padfill[:, :, 0], padfill[:, :, 0], TILE - 1, None, ALU.bitwise_and
                              ).then_inc(pads_masked, 1)
            vec.wait_ge(pads_masked, 1)
            vec.tensor_scalar(padfill[:, :, 0], padfill[:, :, 0], NTOK, None, ALU.add).then_inc(pads_made, 1)
            vec.tensor_copy(prio[:, :], iota_i[:, 0:E])
            vec.tensor_copy(base_e[:, :], iota_i[:, 8:8 + E])
            vec.tensor_copy(run[:, 0, :], iota_i[:, 8:8 + E])
            vec.tensor_copy(tokid[:, :], iota_i[:, 16:16 + GS])
            vec.tensor_copy(tile_no[:, :], iota_i[:, 20:20 + NT]).then_inc(indices_made, 1)
            vec.wait_ge(masks_made, 6)
            vec.wait_ge(indices_made, 1)
            vec.wait_ge(biases_loaded, 16 * 5)

            NORM_STEPS, ROUTE_STEPS = 13, 29
            kinds = {"x norm": (x_step, NORM_STEPS), "attention": (dve_step, 2 * NORM_STEPS + 2), "routing": (route_step, ROUTE_STEPS),
                     "plan": (plan_step, None)}
            state = {}

            def begin(kind, g):
                sem, steps = kinds[kind]
                state.update(sem=sem, g=g, steps=steps, n=0)

            def end():
                assert state["n"] == state["steps"], state

            def link(ins, wait=lambda eng, sem, value: eng.wait_ge(sem, value)):
                state["n"] += 1
                ins.then_inc(state["sem"], 1)
                wait(vec, state["sem"], at(state["g"], state["steps"] or 0, state["n"]))

            def bc(ap, n):
                return ap.unsqueeze(2).to_broadcast([S, GS, n])

            def norm(src, dst, done, ready=lambda s: None):
                for s in range(GS):
                    ready(s)
                    last = vec.bn_stats(stats[0:S, s, :], src[0:S, s, :])
                link(last, wait_apart)
                for s in range(GS):
                    last = vec.bn_aggr(mv[0:S, s, :], stats[0:S, s, :])
                link(last)
                link(vec.tensor_scalar(ve[0:S, :], mv[0:S, :, 1], EPS, None, ALU.add))
                vec.tensor_scalar(hv[0:S, :], ve[0:S, :], -0.5, None, ALU.mult)
                link(vec.tensor_scalar(rs[0:S, :].bitcast(I32), ve[0:S, :].bitcast(I32), -0.5, RSQRT_SEED,
                                       ALU.mult, ALU.add))
                for _ in range(3):
                    link(vec.tensor_tensor(sq[0:S, :], rs[0:S, :], rs[0:S, :], ALU.mult))
                    link(vec.tensor_tensor(sq[0:S, :], sq[0:S, :], hv[0:S, :], ALU.mult))
                    link(vec.scalar_tensor_tensor(rs[0:S, :], sq[0:S, :], 1.5, rs[0:S, :], ALU.add, ALU.mult))
                for s in range(GS):
                    last = vec.tensor_scalar(dst[0:S, s, :], src[0:S, s, :], mv[0:S, s, 0:1], rs[0:S, s:s + 1],
                                             ALU.subtract, ALU.mult)
                last.then_inc(done, 1)

            def norm_x(g):
                begin("x norm", g)
                vec.wait_ge(x_loaded, at(g, 16, 16))
                norm(xin, xin, xhat_ready)
                end()

            def split_low(g, t, first):
                vec.wait_ge(split_hi, at(g, 3, t + 1))
                if first:
                    hi = W[:, 2 * t * PART:(2 * t + 1) * PART]
                    lo = W[:, (2 * t + 1) * PART:(2 * t + 2) * PART]
                else:
                    hi, lo = split[:, 0, :], split[:, 1, :]
                vec.tensor_tensor(lo, stage[:, :], hi, ALU.subtract).then_inc(split_lo, 1)

            def project_bias(g, a):
                vec.wait_ge(A_full[a], at(g, A_USES[a], A_TOK[a] + 1))
                if a == 0:
                    vec.wait_ge(hres_ready, at(g, 1, 0))
                vec.tensor_tensor(hpre[0:S, 2 * a:2 * a + 2, :].rearrange("p s d -> p (s d)"),
                                  psA[a][0:S, :], btok2[0:S, :, :].rearrange("p s d -> p (s d)"),
                                  ALU.add).then_inc(A_free[a], 1)

            def values(g):
                for a in range(2):
                    vec.wait_ge(A_full[a], at(g, A_USES[a], A_V[a] + 1))
                    vec.tensor_tensor(v[0:S, 2 * a:2 * a + 2, :].rearrange("p s d -> p (s d)"),
                                      psA[a][0:S, :], bv2[0:S, :, :].rearrange("p s d -> p (s d)"),
                                      ALU.add).then_inc(A_free[a], 1)

            def score_max(g):
                vec.wait_ge(T_full, at(g, T_USES, T_SC + 1))
                link(vec.tensor_reduce(smax[0:S, :], psT[0:S, 0:GT].rearrange("p (s t) -> p s t", s=GS),
                                       AX, ALU.max))
                vec.tensor_scalar(smax[0:S, :], smax[0:S, :], -D ** -0.5, None, ALU.mult).then_inc(smax_ready, 1)

            def probs_T(g):
                vec.wait_ge(A_full[0], at(g, A0_USES, A0_PT + 1))
                vec.tensor_copy(probT[0:S, :, :].rearrange("p s t -> p (s t)"), psA[0][0:S, 0:GT]
                                ).then_inc(A_free[0], 1)
                vec.wait_ge(T_free, at(g, T_USES, T_SC + 1))
                link(vec.reciprocal(ssum[0:S, :], ssum[0:S, :]))

            def attended(g):
                for a in (1, 0):
                    vec.wait_ge(A_full[a], at(g, A_USES[a], A_PV[a] + 1))
                    for i in range(2):
                        s = 2 * (1 - a) + i
                        last = vec.scalar_tensor_tensor(h2[0:S, s, :], psA[a][0:S, i * D:(i + 1) * D],
                                                        ssum[0:S, s:s + 1], h[0:S, s, :], ALU.mult, ALU.add)
                    last.then_inc(A_free[a], 1)
                vec.wait_ge(A_free[0], at(g, A0_USES, A0_PV + 1))

            def token_rows_low(g):
                vec.wait_ge(rows_hi, at(g, 1, 1))
                vec.tensor_tensor(rows[0:S, :, D:2 * D], xn[0:S, :, :], rows[0:S, :, 0:D], ALU.subtract
                                  ).then_inc(rows_lo, 1)

            def ffn_inputs_low(g):
                for k in range(DC):
                    vec.wait_ge(x2_hi, at(g, DC, k + 1))
                    vec.tensor_tensor(x2T[:, 1, k, :], xnT[:, k, :], x2T[:, 0, k, :], ALU.subtract
                                      ).then_inc(x2_lo, 1)

            top2_steps = [0]

            def router_logits(g):
                begin("routing", g)
                vec.wait_ge(Y_full, at(g, Y_USES, Y_LG + 1))
                logits = psY[0:S, 0:GS * 8].rearrange("p (s e) -> p s e", e=8)[:, :, 0:E]
                link(vec.tensor_reduce(m1[0:S, :], logits, AX, ALU.max))
                vec.tensor_tensor(lg[0:S, :, :], logits, bc(m1[0:S, :], E), ALU.subtract).then_inc(Y_free, 1)

            def top2(g):
                begin("routing", g)
                state["n"] = 1
                vec.wait_ge(e_ready, at(g, 1, 1))
                link(vec.tensor_reduce(r1[0:S, :], pr[0:S, :, :], AX, ALU.add))
                link(vec.reciprocal(r1[0:S, :], r1[0:S, :]))
                link(vec.tensor_tensor(pr[0:S, :, :], pr[0:S, :, :], bc(r1[0:S, :], E), ALU.mult))
                prio_bc = prio[0:S, :].unsqueeze(1).to_broadcast([S, GS, E])
                for top, hot in ((m1, oh1), (m2, oh2)):
                    link(vec.tensor_reduce(top[0:S, :], pr[0:S, :, :], AX, ALU.max))
                    link(vec.tensor_tensor(t7[0:S, :, :], pr[0:S, :, :], bc(top[0:S, :], E), ALU.is_equal))
                    link(vec.tensor_tensor(t7[0:S, :, :], t7[0:S, :, :], prio_bc, ALU.mult))
                    link(vec.tensor_reduce(r1[0:S, :], t7[0:S, :, :], AX, ALU.max))
                    link(vec.tensor_tensor(hot[0:S, :, :], prio_bc, bc(r1[0:S, :], E), ALU.is_equal))
                    if hot is oh1:
                        link(vec.scalar_tensor_tensor(pr[0:S, :, :], oh1[0:S, :, :], -2.0, pr[0:S, :, :],
                                                      ALU.mult, ALU.add))
                vec.tensor_tensor(pick[0:S, :, :], oh1[0:S, :, :], oh2[0:S, :, :], ALU.add).then_inc(pick_ready, 1)
                link(vec.tensor_tensor(r1[0:S, :], m1[0:S, :], m2[0:S, :], ALU.add))
                link(vec.tensor_scalar(r1[0:S, :], r1[0:S, :], 1e-9, None, ALU.add))
                link(vec.reciprocal(r1[0:S, :], r1[0:S, :]))
                vec.wait_ge(meta_stored, at(g, 16 * 2 * GS, 0))
                meta_f = meta[0:S, :, :, :].bitcast(F32)
                for k, top in enumerate((m1, m2)):
                    vec.tensor_tensor(meta_f[:, :, k, 1], top[0:S, :], r1[0:S, :], ALU.mult)
                    last = vec.tensor_copy(meta[0:S, :, k, 0], tokid[0:S, :])
                link(last)
                link(vec.tensor_scalar(tokid[0:S, :], tokid[0:S, :], float(GT), None, ALU.add))
                top2_steps[0] = state["n"]

            def places(g):
                begin("routing", g)
                state["n"] = top2_steps[0]
                vec.wait_ge(Y_full, at(g, Y_USES, Y_RANK + 1))
                rank = psY[0:S, 0:GS * E].rearrange("p (s e) -> p s e", e=E)
                for s in range(GS):
                    link(vec.tensor_tensor(run[0:S, s + 1, :], run[0:S, s, :],
                                           psY[0:S, 64 + s * E:64 + (s + 1) * E], ALU.add))
                vec.tensor_tensor(t7[0:S, :, :], rank, run[0:S, 0:GS, :], ALU.add).then_inc(Y_free, 1)
                vec.wait_ge(Y_free, at(g, Y_USES, Y_RANK + 1))
                for k, hot in enumerate((oh1, oh2)):
                    link(vec.tensor_tensor(hot[0:S, :, :], hot[0:S, :, :], t7[0:S, :, :], ALU.mult))
                    link(vec.tensor_reduce(posf[0:S, :, k], hot[0:S, :, :], AX, ALU.add))
                vec.tensor_copy(pos[0:S, :, :], posf[0:S, :, :]).then_inc(meta_ready, 1)
                link(vec.tensor_copy(run[0:S, 0, :], run[0:S, GS, :]))
                end()

            def ffn_piece(g, c):
                if c < HC:
                    vec.wait_ge(G_free[c % 2], at(g, G_USES[c % 2], c // 2 + 1))
                    vec.wait_ge(U_full[c % 2], at(g, U_USES, c // 2 + 1))
                    vec.tensor_tensor(sil[:, c % 2, 0:GT], psU[c % 2][:, 0:GT], sil[:, c % 2, 0:GT], ALU.mult
                                      ).then_inc(hf_ready, 1)
                if c >= 1:
                    vec.wait_ge(hid_hi, at(g, HC, c))
                    vec.tensor_tensor(hid[:, 1, c - 1, 0:GT], sil[:, (c - 1) % 2, 0:GT], hid[:, 0, c - 1, 0:GT],
                                      ALU.subtract).then_inc(hid_lo, 1)

            def ffn_out(g, s):
                vec.wait_ge(hres_ready, at(g, 1, 1))
                if s == 0:
                    vec.wait_ge(out_stored, at(g, 16, 0))
                if s % 2 == 0:
                    vec.wait_ge(Y_full, at(g, Y_USES, Y_D0 + s // 2 + 1))
                    src, free = psY, Y_free
                else:
                    vec.wait_ge(G_full[0], at(g, G_USES[0], HC // 2 + s // 2 + 1))
                    src, free = psG[0], G_free[0]
                vec.tensor_tensor(yout[0:S, s, :], src[0:S, 0:D], hres[0:S, s, :], ALU.add).then_inc(free, 1)

            def group(g, first=False, last=False):
                ffn = (lambda c: None) if first else (lambda c: ffn_piece(g - 1, c))
                down = (lambda s: None) if first else (lambda s: ffn_out(g - 1, s))
                if not first:
                    router_logits(g - 1)
                ffn(0)
                if not first:
                    top2(g - 1)
                ffn(1)
                split_low(g, 0, first)
                project_bias(g, 0)
                project_bias(g, 1)
                ffn(2)
                begin("attention", g)
                norm(h, xn, xn_ready, lambda s: vec.wait_ge(h_ready, at(g, 2, s // 2 + 1)) if s % 2 == 0 else None)
                for c in range(3, 7):
                    ffn(c)
                split_low(g, 1, first)
                if not last:
                    norm_x(g + 1)
                ffn(7)
                ffn(8)
                values(g)
                if not first:
                    places(g - 1)
                resume(g)
                score_max(g)
                down(0)
                down(1)
                probs_T(g)
                attended(g)
                norm(h2, xn, xn2_ready)
                end()
                down(2)
                down(3)
                split_low(g, 2, first)
                token_rows_low(g)
                ffn_inputs_low(g)

            def resume(g):
                begin("attention", g)
                state["n"] = NORM_STEPS

            norm_x(0)
            group(0, first=True)
            group(1)
            with vec.Fori(2, NG - 1) as g:
                group(g)
            group(NG - 1, last=True)
            router_logits(NG - 1)
            top2(NG - 1)
            places(NG - 1)

            begin("plan", 0)
            link(vec.tensor_tensor(tcount[:, :], run[0:1, 0, :], base_e[0:1, :], ALU.subtract))
            link(vec.tensor_scalar(tcount[:, :], tcount[:, :], float(TILE - 1), None, ALU.add))
            link(vec.tensor_copy(ntile[:, :], tcount[:, :]))
            link(vec.tensor_scalar(ntile[:, :], ntile[:, :], 8, None, ALU.logical_shift_right))
            link(vec.tensor_copy(tcount[:, :], ntile[:, :]))
            link(vec.tensor_copy(tends[:, 0:1], tcount[:, 0:1]))
            for e in range(1, E):
                link(vec.tensor_tensor(tends[:, e:e + 1], tends[:, e - 1:e], tcount[:, e:e + 1], ALU.add))
            vec.tensor_copy(ends_i[:, 0:E], tends[:, :])
            link(vec.tensor_tensor(passed[:, :, :], tile_no[0:1, :].unsqueeze(2).to_broadcast([1, NT, E]),
                                   tends[:, :].unsqueeze(1).to_broadcast([1, NT, E]), ALU.is_ge))
            link(vec.tensor_reduce(ej[:, :], passed[:, :, 0:E - 1], AX, ALU.add))
            link(vec.tensor_tensor(passed[:, :, :], passed[:, :, :],
                                   tcount[:, :].unsqueeze(1).to_broadcast([1, NT, E]), ALU.mult))
            link(vec.tensor_reduce(sj[:, :], passed[:, :, 0:E - 1], AX, ALU.add))
            link(vec.tensor_tensor(sj[:, :], tile_no[0:1, :], sj[:, :], ALU.subtract))
            link(vec.scalar_tensor_tensor(sj[:, :], ej[:, :], float(REGION // TILE), sj[:, :], ALU.mult, ALU.add))
            vec.tensor_copy(plan[:, 2, :], sj[:, :])
            link(vec.tensor_scalar(ej[:, :], ej[:, :], 1.0, None, ALU.add))
            vec.tensor_scalar(plan[:, 1, :], ej[:, :], 16.0, None, ALU.mult)
            for n in range(NS, NE, NS):
                link(vec.tensor_scalar(tj[:, :], ej[:, :], float(NS), float(-NS), ALU.is_ge, ALU.mult))
                link(vec.tensor_tensor(ej[:, :], ej[:, :], tj[:, :], ALU.add))
            vec.tensor_scalar(plan[:, 0, :], ej[:, :], float(SLOT), None, ALU.mult).then_inc(plan_ready, 1)

            for c in range(HC + 1):
                ffn_piece(NG - 1, c)
            for s in range(GS):
                ffn_out(NG - 1, s)

            def tile_T(j, b):
                vec.wait_ge(T_full, at(j, 1, 1) + NG * T_USES)
                vec.tensor_copy(gxT[:, b, :, :, :].rearrange("p a k t -> p (a k t)"), psT_b).then_inc(T_free, 1)

            def tile_piece(j, b, q):
                Q = HC // 2
                if q < Q:
                    vec.wait_ge(G_free[q % 2], at(j, Q // 2, q // 2 + 1) + NG * G_USES[q % 2])
                    vec.wait_ge(U_full[q % 2], at(j, Q // 2, q // 2 + 1) + NG * U_USES)
                    vec.tensor_tensor(sil[:, q % 2, :], psU[q % 2][:, :], sil[:, q % 2, :], ALU.mult
                                      ).then_inc(hf_ready, 1)
                if q >= 1:
                    vec.wait_ge(hid_hi, at(j, Q, q) + NG * HC)
                    vec.tensor_tensor(hidr[:, b, 1, 2 * q - 2:2 * q, :],
                                      sil[:, (q - 1) % 2, :].rearrange("p (c t) -> p c t", c=2),
                                      hidr[:, b, 0, 2 * q - 2:2 * q, :], ALU.subtract).then_inc(hid_lo, 1)

            def tile_out(j, b, k):
                vec.wait_ge(Y_full, at(j, SUB, k + 1) + NG * Y_USES)
                vec.wait_ge(smeta_ready, at(j, 1, 1))
                vec.tensor_scalar(ysb[:, b, k, :], psY[:, 0:D], smeta[:, b, k, 1:2].bitcast(F32), None, ALU.mult
                                  ).then_inc(Y_free, 1)

            def routed_tile(j, b, older, newer):
                tile_piece(j, b, 0)
                tile_piece(j, b, 1)
                if older:
                    tile_out(j - 1, 1 - b, 0)
                tile_piece(j, b, 2)
                if newer:
                    tile_T(j + 1, 1 - b)
                tile_piece(j, b, 3)
                tile_piece(j, b, 4)
                if older:
                    tile_out(j - 1, 1 - b, 1)

            tile_T(0, 0)
            routed_tile(0, 0, False, True)
            routed_tile(1, 1, True, True)
            with vec.Fori(1, NT // 2 - 1) as i:
                for b in range(2):
                    routed_tile(i * 2 + b, b, True, True)
            routed_tile(NT - 2, 0, True, True)
            routed_tile(NT - 1, 1, True, False)
            for k in range(SUB):
                tile_out(NT - 1, 1, k)

        @block.tensor
        def _(pe):
            pe.wait_ge(masks_made, 6)
            pe.wait_ge(consts_loaded, 48)

            def transposes(g, where, src):
                bank_, full, free, uses, use = where
                pe.wait_ge(free, at(g, uses, use))
                for s in range(GS):
                    last = pe.transpose(bank_[:, s * S:(s + 1) * S], src(s), ident[0:S, 0:S])
                last.then_inc(full, 1)

            def written(g, where):
                for bank_, full, free, uses, use in where:
                    pe.wait_ge(free, at(g, uses, use + 1))

            def x_T(g, k):
                transposes(g, X_AT[k], lambda s: xin[0:S, s, k * P:(k + 1) * P])

            def xn_T(g, k, where):
                transposes(g, where[k], lambda s: xn[0:S, s, k * P:(k + 1) * P])

            def project(g):
                written(g, X_AT)
                for a in range(2):
                    pe.wait_ge(A_free[a], at(g, A_USES[a], A_TOK[a]))
                    for i in range(2):
                        s = 2 * a + i
                        for k in range(FC):
                            last = pe.matmul(psA[a][0:S, i * D:(i + 1) * D], yT[:, k, s * S:(s + 1) * S],
                                             wtok[:, k, :], start=(k == 0), stop=(k == FC - 1))
                    last.then_inc(A_full[a], 1)

            def queries_keys(g, w):
                if w == 0:
                    written(g, XN_AT)
                for m in range(DC):
                    pe.wait_ge(A_free[m], at(g, A_USES[m], A_QK[w][m]))
                    for k in range(DC):
                        last = pe.matmul(psA[m][:, 0:GT], wqkv[:, w, k, m * P:(m + 1) * P], xnT[:, k, :],
                                         start=(k == 0), stop=(k == DC - 1))
                    last.then_inc(A_full[m], 1)

            def values(g):
                for a in range(2):
                    pe.wait_ge(A_free[a], at(g, A_USES[a], A_V[a]))
                    for i in range(2):
                        s = 2 * a + i
                        for k in range(DC):
                            last = pe.matmul(psA[a][0:S, i * D:(i + 1) * D], xnT[:, k, s * S:(s + 1) * S],
                                             wqkv[:, 2, k, :], start=(k == 0), stop=(k == DC - 1))
                    last.then_inc(A_full[a], 1)

            def scores(g):
                for m in range(DC):
                    pe.wait_ge(A_free[m], at(g, A_USES[m], A_QK[1][m] + 1))
                pe.wait_ge(T_free, at(g, T_USES, T_SC))
                for s in range(GS):
                    for m in range(DC):
                        last = pe.matmul(psT[0:S, s * S:(s + 1) * S], qT[:, m, s * S:(s + 1) * S],
                                         kT[:, m, s * S:(s + 1) * S], start=(m == 0), stop=(m == DC - 1))
                last.then_inc(T_full, 1)

            def probs_T(g):
                pe.wait_ge(T_free, at(g, T_USES, T_SC + 1))
                pe.wait_ge(A_free[0], at(g, A0_USES, A0_PT))
                for s in range(GS):
                    last = pe.transpose(psA[0][0:S, s * S:(s + 1) * S], prob[0:S, s, :], ident[0:S, 0:S])
                last.then_inc(A_full[0], 1)

            def attend(g):
                pe.wait_ge(A_free[0], at(g, A0_USES, A0_PT + 1))
                for a in (1, 0):
                    pe.wait_ge(A_free[a], at(g, A_USES[a], A_PV[a]))
                    for i in range(2):
                        s = 2 * (1 - a) + i
                        last = pe.matmul(psA[a][0:S, i * D:(i + 1) * D], probT[0:S, s, :], v[0:S, s, :],
                                         start=True, stop=True)
                    last.then_inc(A_full[a], 1)

            def router(g):
                written(g, H_AT)
                pe.wait_ge(T_free, at(g, T_USES, T_LT))
                for k in range(DC):
                    last = pe.matmul(psT[0:E, 0:GT], wrt[:, k, :], xnT[:, k, :], start=(k == 0),
                                     stop=(k == DC - 1))
                last.then_inc(T_full, 1)

            def logits(g):
                pe.wait_ge(T_free, at(g, T_USES, T_LT + 1))
                wait_apart(pe, Y_free, at(g, Y_USES, Y_LG))
                for s in range(GS):
                    last = pe.transpose(psY[0:S, s * 8:s * 8 + E], logT[:, s * S:(s + 1) * S], ident[0:E, 0:E])
                last.then_inc(Y_full, 1)

            def ranks(g):
                pe.wait_ge(pick_ready, at(g, 1, 1))
                pe.wait_ge(Y_free, at(g, Y_USES, Y_RANK))
                picks = pick[0:S, :, :].rearrange("p s e -> p (s e)")
                pe.matmul(psY[0:S, 0:GS * E], before[0:S, 0:S], picks, start=True, stop=True)
                pe.matmul(psY[0:S, 64:64 + GS * E], ones_b[0:S, 0:S], picks, start=True, stop=True
                          ).then_inc(Y_full, 1)

            def ffn_piece(g, c):
                if c == 0:
                    pe.wait_ge(x2_hi, at(g, DC, DC))
                    pe.wait_ge(x2_lo, at(g, DC, DC))
                for which, ps, full in ((0, psG, G_full), (1, psU, U_full)):
                    if which == 0:
                        pe.wait_ge(G_free[c % 2], at(g, G_USES[c % 2], c // 2))
                    else:
                        pe.wait_ge(hf_ready, at(g, HC, max(c - 1, 0)))
                    n = 0
                    for wp, xp in TERMS:
                        for k in range(DC):
                            last = pe.matmul(ps[c % 2][:, 0:GT], wcols(0, which, wp, k * DFF + c * P, P),
                                             x2T[:, xp, k, :], start=(n == 0), stop=(n == 3 * DC - 1))
                            n += 1
                    last.then_inc(full[c % 2], 1)

            def ffn_down(g, s):
                if s == 0:
                    pe.wait_ge(hid_hi, at(g, HC, HC))
                    pe.wait_ge(hid_lo, at(g, HC, HC))
                if s % 2 == 0:
                    pe.wait_ge(Y_free, at(g, Y_USES, Y_D0 + s // 2))
                    dst, full = psY, Y_full
                else:
                    pe.wait_ge(G_free[0], at(g, G_USES[0], HC // 2 + s // 2))
                    dst, full = psG[0], G_full[0]
                n = 0
                for wp, xp in TERMS:
                    for c in range(HC):
                        last = pe.matmul(dst[0:S, 0:D], hid[:, xp, c, s * S:(s + 1) * S],
                                         wcols(0, 2, wp, c * D, D), start=(n == 0), stop=(n == 3 * HC - 1))
                        n += 1
                last.then_inc(full, 1)

            def group(g, first=False):
                ffn = (lambda c: None) if first else (lambda c: ffn_piece(g - 1, c))
                down = (lambda s: None) if first else (lambda s: ffn_down(g - 1, s))
                pe.wait_ge(xhat_ready, at(g, 1, 1))
                x_T(g, 0)
                x_T(g, 1)
                if not first:
                    logits(g - 1)
                ffn(0)
                x_T(g, 2)
                x_T(g, 3)
                ffn(1)
                project(g)
                for c in range(2, 6):
                    ffn(c)
                pe.wait_ge(xn_ready, at(g, 1, 1))
                xn_T(g, 0, XN_AT)
                xn_T(g, 1, XN_AT)
                ffn(6)
                queries_keys(g, 0)
                queries_keys(g, 1)
                ffn(7)
                values(g)
                scores(g)
                if not first:
                    ranks(g - 1)
                down(0)
                down(1)
                probs_T(g)
                attend(g)
                down(2)
                down(3)
                pe.wait_ge(xn2_ready, at(g, 1, 1))
                xn_T(g, 0, H_AT)
                xn_T(g, 1, H_AT)
                router(g)

            group(0, True)
            pe.wait_ge(split_lo, 3)
            group(1)
            with pe.Fori(2, NG) as g:
                group(g)
            logits(NG - 1)
            for c in range(HC):
                ffn_piece(NG - 1, c)
                if c == 1:
                    ranks(NG - 1)
            for s in range(GS):
                ffn_down(NG - 1, s)

            pe.wait_ge(plan_ready, 1)

            def tile_T(j, b):
                pe.wait_ge(grow_loaded, at(j, 16 * SUB, 16 * SUB))
                pe.wait_ge(T_free, at(j, 1, 0) + NG * T_USES)
                for a in range(2):
                    for k in range(DC):
                        for r in range(SUB):
                            last = pe.transpose(psT_b[:, ((a * DC + k) * SUB + r) * P:((a * DC + k) * SUB + r + 1) * P],
                                                grow[:, b, r, (a * DC + k) * P:(a * DC + k + 1) * P], ident_b[:, :])
                last.then_inc(T_full, 1)

            def tile_piece(j, b, q, slot_at):
                Q = HC // 2
                if q == 0:
                    pe.wait_ge(T_free, at(j, 1, 1) + NG * T_USES)
                for which, ps, full in ((0, psG, G_full), (1, psU, U_full)):
                    if which == 0:
                        pe.wait_ge(G_free[q % 2], at(j, Q // 2, q // 2) + NG * G_USES[q % 2])
                    else:
                        pe.wait_ge(hf_ready, at(j, Q, max(q - 1, 0)) + NG * HC)
                    for i in range(2):
                        c = 2 * q + i
                        n = 0
                        for wp, xp in TERMS:
                            for k in range(DC):
                                last = pe.matmul(ps[q % 2][:, i * TILE:(i + 1) * TILE],
                                                 wcols(slot_at, which, wp, k * DFF + c * P, P),
                                                 gxT[:, b, xp, k, :], start=(n == 0), stop=(n == 3 * DC - 1))
                                n += 1
                    last.then_inc(full[q % 2], 1)

            def tile_down(j, b, r, slot_at):
                if r == 0:
                    pe.wait_ge(hid_hi, at(j, HC // 2, HC // 2) + NG * HC)
                    pe.wait_ge(hid_lo, at(j, HC // 2, HC // 2) + NG * HC)
                pe.wait_ge(Y_free, at(j, SUB, r) + NG * Y_USES)
                n = 0
                for wp, xp in TERMS:
                    for c in range(HC):
                        last = pe.matmul(psY[:, 0:D], hidr[:, b, xp, c, r * P:(r + 1) * P],
                                         wcols(slot_at, 2, wp, c * D, D), start=(n == 0), stop=(n == 3 * HC - 1))
                        n += 1
                last.then_inc(Y_full, 1)

            def slot_of(j):
                return pe.value_load(plan[0:1, 0, bass.ds(j, 1)], min_val=0, max_val=(NS - 1) * SLOT)

            def routed_tile(j, b, older, newer):
                loads = pe.value_load(plan[0:1, 1, bass.ds(j, 1)], min_val=16, max_val=16 * E)
                here = slot_of(j)
                pe.wait_ge(expert_loaded, loads)
                tile_piece(j, b, 0, here)
                tile_piece(j, b, 1, here)
                if older:
                    tile_down(j - 1, 1 - b, 0, slot_of(j - 1))
                tile_piece(j, b, 2, here)
                if newer:
                    tile_T(j + 1, 1 - b)
                tile_piece(j, b, 3, here)
                if older:
                    tile_down(j - 1, 1 - b, 1, slot_of(j - 1))

            tile_T(0, 0)
            routed_tile(0, 0, False, True)
            routed_tile(1, 1, True, True)
            with pe.Fori(1, NT // 2 - 1) as i:
                for b in range(2):
                    routed_tile(i * 2 + b, b, True, True)
            routed_tile(NT - 2, 0, True, True)
            routed_tile(NT - 1, 1, True, False)
            for r in range(SUB):
                tile_down(NT - 1, 1, r, slot_of(NT - 1))


def kernel(**inputs):
    import numpy as np
    import concourse.bacc as bacc
    from concourse.bass_utils import run_bass_kernel_spmd

    a = {k: np.asarray(t) for k, t in inputs.items()}

    def ffn_layout(gate, up, down):
        return np.stack([w.T.reshape(-1, P, w.shape[0]).transpose(1, 0, 2).reshape(P, -1)
                         for w in (gate, up, down)])

    ffn = [ffn_layout(a["L0_ffn_shared_gate"], a["L0_ffn_shared_up"], a["L0_ffn_shared_down"])]
    for e in range(E):
        ffn.append(ffn_layout(a["L0_ffn_routed_gate"][e], a["L0_ffn_routed_up"][e], a["L0_ffn_routed_down"][e]))
    arrays = {
        "in_x": a["x"].reshape(B, S, FAN),
        "in_columns": np.concatenate([a[k].reshape(-1, P).T for k in (
            "L0_tok_ln_gamma", "L0_tok_ln_beta", "L0_attn_b_q", "L0_attn_b_k")], axis=1),
        "in_w_tok": np.ascontiguousarray(a["L0_tok_W"].T),
        "in_b_tok": a["L0_tok_b"],
        "in_w_qkv": np.stack([a["L0_attn_W_q"], a["L0_attn_W_k"], a["L0_attn_W_v"]]),
        "in_b_v": a["L0_attn_b_v"],
        "in_w_ffn": np.stack(ffn),
        "in_w_router": np.ascontiguousarray(a["L0_ffn_router_w"].T),
    }
    nc = bacc.Bacc("TRN2", target_bir_lowering=False, num_devices=1)
    args = [nc.dram_tensor(n, t.shape, mybir.dt.from_np(t.dtype), kind="ExternalInput").ap()
            for n, t in arrays.items()]
    out = nc.dram_tensor("out", (NTOK + TILE, D), F32, kind="ExternalOutput").ap()
    audio_tower(nc, *args, out)
    r = run_bass_kernel_spmd(nc, [arrays], core_ids=[0])
    return r.results[0]["out"][:NTOK].reshape(B, S, D)
```

```python
from contextlib import ExitStack

import concourse.bass as bass
from concourse import mybir

F32 = mybir.dt.float32
BF16 = mybir.dt.bfloat16
I32 = mybir.dt.int32
F32R = mybir.dt.float32r
ALU = mybir.AluOpType
ACT = mybir.ActivationFunctionType
AX = mybir.AxisListType.X

P = 128
B, T_IN, C = 32, 250, 256
FAN = 2 * C
S = T_IN // 2
NTOK = B * S
D = 256
DC = D // P
FC = FAN // P
DFF = 1024
HC = DFF // P
E = 7
NE = E + 1
GS = 4
NG = B // GS
GT = GS * S

TILE = 256
SUB = TILE // P
NT = (2 * NTOK + E * (TILE - 1)) // TILE
MIN_T = -(-2 * NTOK // TILE)
PLANNED = NT + 4
REGION = 4096
TABLE = (E - 1) * REGION + PLANNED * TILE
NS = 3
PART = 2048
SLOT = 3 * 2 * PART
EPS = 1e-5
RSQRT_SEED = float(0x5F3759DF)

assert MIN_T % 4 == 0 and NTOK <= REGION and TABLE % P == 0 and NG == E + 1


def audio_tower(nc, x, columns, w_tok, b_tok, w_qkv, b_v, w_ffn, w_router, out):
    with ExitStack() as ctx:
        def sb(name, shape, dt=F32):
            return ctx.enter_context(nc.sbuf_tensor(name, shape, dt))

        def bank(name):
            return ctx.enter_context(nc.psum_tensor(name, [P, 512], F32))

        def sem(name):
            return ctx.enter_context(nc.semaphore(name))

        token_rows = nc.dram_tensor("token_rows", [NTOK, 2 * D], BF16).ap()
        choices = nc.dram_tensor("choices", [TABLE, 2], I32).ap()
        split_ffn = nc.dram_tensor("split_ffn", [E, 3, P, 2 * PART], BF16).ap()

        ident = sb("ident", [P, P])
        ident_b = sb("ident_b", [P, P], BF16)
        before = sb("before", [P, P], BF16)
        ones_b = sb("ones_b", [P, P], BF16)
        wtok = sb("wtok", [P, FC, D])
        wqkv = sb("wqkv", [P, 2, 3, DC, D], F32R)
        wrt = sb("wrt", [P, DC, E])
        cols = sb("cols", [P, 2 * FC + 2 * DC])
        gam, bet = cols[:, 0:FC], cols[:, FC:2 * FC]
        bqk = cols[:, 2 * FC:].rearrange("p (w c) -> p w c", w=2)
        btok2 = sb("btok2", [P, 2, D])
        bv2 = sb("bv2", [P, 2, D])
        prio = sb("prio", [P, E])
        base_e = sb("base_e", [P, E])
        tokid = sb("tokid", [P, GS])
        iota_i = sb("iota_i", [P, 64], I32)
        tile_no = sb("tile_no", [P, PLANNED])

        xin = sb("xin", [P, GS, FAN])
        hpre = sb("hpre", [P, GS, D])
        h = sb("h", [P, GS, D])
        xn = sb("xn", [P, GS, D])
        xn_parts = sb("xn_parts", [P, 2, DC, GT], F32R)
        xnT = sb("xnT", [P, DC, GT])
        h2 = hpre
        stats = sb("stats", [P, GS, 6])
        mv = sb("mv", [P, GS, 2])
        ve = sb("ve", [P, GS])
        hv = sb("hv", [P, GS])
        rs = sb("rs", [P, GS])
        sq = sb("sq", [P, GS])
        x_scale = sb("x_scale", [P, GS])
        x_shift = sb("x_shift", [P, GS])
        smax = sb("smax", [P, GS])
        unused = sb("unused", [P, 1])
        ssum = sb("ssum", [P, GS])
        logT = sb("logT", [E, GT])
        lg = sb("lg", [P, GS, E])
        pr = sb("pr", [P, GS, E])
        t7 = sb("t7", [P, GS, E])
        oh1 = sb("oh1", [P, GS, E])
        oh2 = sb("oh2", [P, GS, E])
        pick = sb("pick", [P, GS, E], BF16)
        run = sb("run", [P, GS + 1, E])
        m1 = sb("m1", [P, GS])
        m2 = sb("m2", [P, GS])
        r1 = sb("r1", [P, GS])
        posf = sb("posf", [P, GS, 2])
        pos = sb("pos", [P, GS, 2], I32)
        meta = sb("meta", [P, GS, 2, 2], I32)
        rows = sb("rows", [P, GS, 2 * D], BF16)
        x2T = sb("x2T", [P, 2, DC, GT], BF16)
        hres = sb("hres", [P, GS, D])
        yout = sb("yout", [P, GS, D])
        hid = sb("hid", [P, 2, HC, 512], BF16)
        hidr = hid[:].rearrange("p a c (b t) -> p b a c t", b=2)
        sil = sb("sil", [P, 2, 512])
        stage = sb("stage", [P, PART])
        split = sb("split", [P, 2, PART], BF16)
        W = sb("W", [P, NS * SLOT], BF16)
        last_slot = W[:, (NS - 1) * SLOT:NS * SLOT].bitcast(F32)
        yT = last_slot[:, 0:FC * GT].rearrange("p (k t) -> p k t", k=FC)
        qT, kT = [last_slot[:, (FC + DC * i) * GT:(FC + DC * (i + 1)) * GT].rearrange("p (k t) -> p k t", k=DC)
                  for i in range(2)]
        prob, probT = [last_slot[:, (FC + 2 * DC + i) * GT:(FC + 2 * DC + i + 1) * GT].rearrange(
            "p (s t) -> p s t", s=GS) for i in range(2)]
        v_at = (FC + 2 * DC + 2) * GT
        v = last_slot[:, v_at:v_at + GS * D].rearrange("p (s d) -> p s d", s=GS)
        staged = hid[:].rearrange("p a c t -> p (a c t)").bitcast(F32)
        wqkv_staged = staged[:, 0:3 * DC * D].rearrange("p (w k n) -> p w k n", w=3, k=DC)
        grow = sb("grow", [P, 2, SUB, 2 * D], BF16)
        gxT = sb("gxT", [P, 2, 2, DC, TILE], BF16)
        gmeta = sb("gmeta", [P, 2, SUB, 2], I32)
        smeta = sb("smeta", [P, 2, SUB, 2], I32)
        gidx = sb("gidx", [P, 2, SUB], I32)
        ysb = sb("ysb", [P, 2, SUB, D])
        ntile = sb("ntile", [1, E], I32)
        tends = sb("tends", [1, E])
        tcount = sb("tcount", [1, E])
        ends_i = sb("ends_i", [1, 8], I32)
        passed = sb("passed", [1, PLANNED, E])
        ej = sb("ej", [1, PLANNED])
        sj = sb("sj", [1, PLANNED])
        tj = sb("tj", [1, PLANNED])
        plan = sb("plan", [1, 3, PLANNED], I32)
        padfill = grow[:].rearrange("p a b c -> p (a b c)").bitcast(I32)[
            :, 0:TABLE // P * 2].rearrange("p (r w) -> p r w", w=2)

        psT, psA0, psA1, psY = bank("psT"), bank("psA0"), bank("psA1"), bank("psY")
        psG = [bank("psG0"), bank("psG1")]
        psU = [bank("psU0"), bank("psU1")]
        psA = [psA0, psA1]
        psT_b = psT[:, :].bitcast(BF16)

        T_full, T_free = sem("T_full"), sem("T_free")
        A_full, A_free = [sem("A0_full"), sem("A1_full")], [sem("A0_free"), sem("A1_free")]
        Y_full, Y_free = sem("Y_full"), sem("Y_free")
        G_full, G_free = [sem("G0_full"), sem("G1_full")], [sem("G0_free"), sem("G1_free")]
        U_full = [sem("U0_full"), sem("U1_full")]
        T_XN0, T_SC, T_H0, T_LT, T_USES = range(5)
        A0_X0, A0_X2, A0_TOK, A0_Q, A0_K, A0_V, A0_PT, A0_PV, A0_USES = range(9)
        A1_X1, A1_X3, A1_TOK, A1_XN1, A1_Q, A1_K, A1_V, A1_PV, A1_USES = range(9)
        Y_LG, Y_RANK, Y_D1, Y_USES = range(4)
        G_USES, U_USES = [HC // 2 + 2, HC // 2 + 2], HC // 2
        G_GATE = (0, 1)
        A_USES, A_TOK, A_V, A_PV = (A0_USES, A1_USES), (A0_TOK, A1_TOK), (A0_V, A1_V), (A0_PV, A1_PV)
        A_QK = ((A0_Q, A1_Q), (A0_K, A1_K))
        IN_T, IN_A0, IN_A1 = ((psT, T_full, T_free, T_USES), (psA0, A_full[0], A_free[0], A0_USES),
                              (psA1, A_full[1], A_free[1], A1_USES))
        X_AT = [(*IN_A0, A0_X0), (*IN_A1, A1_X1), (*IN_A0, A0_X2), (*IN_A1, A1_X3)]
        XN_AT = [(*IN_T, T_XN0), (*IN_A1, A1_XN1)]
        H_AT = [(*IN_T, T_H0), (psG[1], G_full[1], G_free[1], G_USES[1], 0)]
        DOWN_AT = [(psG[0], G_full[0], G_free[0], G_USES[0], HC // 2), (psY, Y_full, Y_free, Y_USES, Y_D1),
                   (psG[1], G_full[1], G_free[1], G_USES[1], HC // 2 + 1),
                   (psG[0], G_full[0], G_free[0], G_USES[0], HC // 2 + 1)]

        consts_high, consts_low, xn_high = sem("consts_high"), sem("consts_low"), sem("xn_high")
        consts_loaded, masks_made, biases_loaded = sem("consts_loaded"), sem("masks_made"), sem("biases_loaded")
        iota_made, indices_made = sem("iota_made"), sem("indices_made")
        pads_masked, pads_made, pads_stored = sem("pads_masked"), sem("pads_made"), sem("pads_stored")
        x_loaded, x_moments, xhat_ready = sem("x_loaded"), sem("x_moments"), sem("xhat_ready")
        h_ready, xn_ready = sem("h_ready"), sem("xn_ready")
        smax_ready = sem("smax_ready")
        hres_ready, xn2_ready = sem("hres_ready"), sem("xn2_ready")
        rows_hi, rows_lo, rows_stored = sem("rows_hi"), sem("rows_lo"), sem("rows_stored")
        x2_hi, x2_lo = sem("x2_hi"), sem("x2_lo")
        e_ready = sem("e_ready")
        pick_ready, meta_ready, meta_stored = sem("pick_ready"), sem("meta_ready"), sem("meta_stored")
        dve_step, x_step, route_step = sem("dve_step"), sem("x_step"), sem("route_step")
        plan_step, passed_by = sem("plan_step"), sem("passed_by")
        hf_ready, hid_hi, hid_lo = sem("hf_ready"), sem("hid_hi"), sem("hid_lo")
        out_stored = sem("out_stored")
        stage_loaded, split_hi, split_lo, split_stored = (
            sem("stage_loaded"), sem("split_hi"), sem("split_lo"), sem("split_stored"))
        rows_planned, plan_ready, expert_loaded = sem("rows_planned"), sem("plan_ready"), sem("expert_loaded")
        gmeta_loaded, gidx_ready, grow_loaded = sem("gmeta_loaded"), sem("gidx_ready"), sem("grow_loaded")
        smeta_ready, added = sem("smeta_ready"), sem("added")

        def at(g, per_group, n):
            return g * per_group + n

        def wait_apart(eng, sem, value):
            eng.wait_ge(sem, value).then_inc(passed_by, 1)

        def wcols(slot_at, which, part, first, n):
            return W[:, bass.ds(slot_at + (2 * which + part) * PART + first, n)]

        def tile_count(eng):
            eng.wait_ge(plan_ready, 1)
            return eng.value_load(ends_i[0:1, E - 1:E], min_val=MIN_T, max_val=NT)

        def steps_that_vary(eng, tiles, step, tail=None):
            with eng.Fori(MIN_T // 2, NT // 2 + 1) as i:
                for b in range(2):
                    j = i * 2 + b
                    with eng.If(j < tiles):
                        step(j, b)
                    if tail is not None:
                        with eng.If(j < tiles + 1):
                            with eng.If(j > tiles - 1):
                                tail(j, b)

        TERMS = ((0, 0), (0, 1), (1, 0))
        x_groups = x.rearrange("(g s) p f -> g p s f", s=GS)
        out_groups = out[0:NTOK, :].rearrange("(g s p) d -> g p s d", s=GS, p=S)
        rows_groups = token_rows.rearrange("(g s p) d -> g p s d", s=GS, p=S)
        w_stage = w_ffn.rearrange("e t p n -> (e t) p n")
        split_steps = split_ffn.rearrange("e t p n -> (e t) p n")
        choice_tiles = choices.rearrange("(r p k) w -> r p (k w)", p=P, k=SUB)

        block = ctx.enter_context(nc.Block())

        @block.sync
        def _(sp):
            def load_stage(step):
                sp.dma_start(stage[:, :], w_stage[step, :, :]).then_inc(stage_loaded, 16)

            def load_x(g):
                sp.dma_start(xin[0:S, :, :], x_groups[g, :, :, :]).then_inc(x_loaded, 16)

            def split_traffic(g, first):
                for t in range(3):
                    if t == 2 and not first:
                        store_rows(g)
                        store_out(g - 1)
                    sp.wait_ge(split_lo, at(g, 3, t + 1))
                    load_stage(g * 3 + t + 1)
                    if not first:
                        sp.dma_start(split_steps[(g - 1) * 3 + t, :, :],
                                     split[:, :, :].rearrange("p a n -> p (a n)")).then_inc(split_stored, 16)

            load_x(0)
            sp.dma_start(wtok[:, :, :], w_tok.rearrange("(c p) n -> p c n", p=P)).then_inc(consts_loaded, 16)
            sp.dma_start(wqkv_staged, w_qkv.rearrange("w (c p) n -> p w c n", p=P)).then_inc(consts_loaded, 16)
            sp.dma_start(wrt[:, :, :], w_router.rearrange("(c p) n -> p c n", p=P)).then_inc(consts_loaded, 16)
            load_stage(0)

            def load_expert(n):
                if n > 1:
                    sp.wait_ge(expert_loaded, 16 * (n - 1))
                sp.dma_start(
                    W[:, (n % NS) * SLOT:(n % NS + 1) * SLOT].rearrange("p (t n) -> p t n", t=3),
                    split_ffn[n - 1, :, :, :].rearrange("t p n -> p t n")).then_inc(expert_loaded, 16)

            def store_rows(g):
                sp.wait_ge(rows_hi, at(g, 1, 1))
                sp.wait_ge(rows_lo, at(g, 1, 1))
                sp.dma_start(rows_groups[g, :, :, :], rows[0:S, :, :]).then_inc(rows_stored, 16)

            def rest_of_group(g, first=False):
                sp.wait_ge(A_full[1], at(g, A1_USES, A1_X3 + 1))
                load_x(g + 1)
                split_traffic(g, first)
                if first:
                    store_rows(g)

            def store_out(g):
                sp.wait_ge(Y_free, at(g, Y_USES, Y_USES))
                for i in range(2):
                    sp.wait_ge(G_free[i], at(g, G_USES[i], G_USES[i]))
                sp.dma_start(out_groups[g, :, :, :], yout[0:S, :, :]).then_inc(out_stored, 16)

            rest_of_group(0, first=True)
            rest_of_group(1)
            with sp.Fori(2, NG - 1) as g:
                rest_of_group(g)
            sp.wait_ge(split_stored, 16 * 3 * (NG - 2))
            for t in range(3):
                if t == 1:
                    load_expert(1)
                if t == 2:
                    store_rows(NG - 1)
                    store_out(NG - 2)
                    load_expert(2)
                sp.wait_ge(split_lo, (NG - 1) * 3 + t + 1)
                if t < 2:
                    load_stage((NG - 1) * 3 + t + 1)
                sp.dma_start(split_steps[(NG - 2) * 3 + t, :, :],
                             split[:, :, :].rearrange("p a n -> p (a n)")).then_inc(split_stored, 16)

            sp.wait_ge(split_stored, 16 * 3 * E)
            for n in range(NS, NE):
                if n == NS:
                    store_out(NG - 1)
                if n == NS + 1:
                    sp.wait_ge(plan_ready, 1)
                if n > NS:
                    ended = sp.value_load(ends_i[0:1, n - NS - 1:n - NS], min_val=0, max_val=NT)
                    sp.wait_ge(Y_full, ended * SUB + NG * Y_USES)
                load_expert(n)
            sp.wait_ge(out_stored, 16 * NG)
            wait_apart(sp, added, tile_count(sp) * (16 * SUB))
            sp.wait_ge(expert_loaded, 16 * E)

        @block.gpsimd
        def _(pool):
            def iota(dst, pattern, base, mult):
                pool.iota(dst, pattern, base=base, channel_multiplier=mult).then_inc(iota_made, 1)

            pool.memset(ident[:, :], 0.0).then_inc(masks_made, 1)
            pool.memset(before[:, :], 1.0).then_inc(masks_made, 1)
            pool.memset(ones_b[:, :], 1.0).then_inc(masks_made, 1)
            pool.wait_ge(masks_made, 3)
            pool.affine_select(out=ident[:, :], in_=ident[:, :], compare_op=ALU.not_equal, fill=1.0, base=0,
                               pattern=[[-1, P]], channel_multiplier=1).then_inc(masks_made, 1)
            pool.affine_select(out=before[:, :], in_=before[:, :], compare_op=ALU.is_gt, fill=0.0, base=0,
                               pattern=[[1, P]], channel_multiplier=-1).then_inc(masks_made, 1)
            pool.wait_ge(masks_made, 5)
            pool.tensor_copy(ident_b[:, :], ident[:, :]).then_inc(masks_made, 1)
            pool.memset(yout[:, 0:2, :], 0.0).then_inc(pads_made, 1)
            pool.memset(padfill[:, :, 1], 0).then_inc(pads_made, 1)
            iota(padfill[:, :, 0], [[1, TABLE // P]], 0, TABLE // P)
            iota(iota_i[:, 0:E], [[-1, E]], E, 0)
            iota(iota_i[:, 8:8 + E], [[REGION, E]], 0, 0)
            iota(iota_i[:, 16:16 + GS], [[S, GS]], 0, 1)
            iota(iota_i[:, 20:20 + PLANNED], [[1, PLANNED]], 0, 0)
            pool.wait_ge(pads_made, 3)
            pool.dma_start(choices.rearrange("(p r) w -> p r w", p=P), padfill).then_inc(pads_stored, 16)
            pool.dma_start(out[NTOK:NTOK + TILE, :].rearrange("(k p) d -> p k d", p=P), yout[:, 0:2, :]
                           ).then_inc(pads_stored, 16)
            pool.wait_ge(pads_stored, 32)

            def residual(g, first):
                wait_apart(pool, A_free[0], at(g, A0_USES, A0_PV + 1))
                if not first:
                    wait_apart(pool, G_free[0], at(g - 1, G_USES[0], G_USES[0]))
                pool.tensor_copy(hres[0:S, :, :], h2[0:S, :, :]).then_inc(hres_ready, 1)

            def store_choices(g):
                wait_apart(pool, meta_ready, at(g, 1, 1))
                for s in range(GS):
                    for k in range(2):
                        pool.indirect_dma_start(
                            choices[:, :], bass.IndirectOffsetOnAxis(ap=pos[0:S, s, k:k + 1], axis=0),
                            meta[0:S, s, k, :], None).then_inc(meta_stored, 16)

            residual(0, True)
            store_choices(0)
            residual(1, False)
            store_choices(1)
            with pool.Fori(2, NG) as g:
                residual(g, False)
                store_choices(g)

            pool.wait_ge(rows_planned, 1)
            pool.wait_ge(meta_stored, 16 * 2 * GS * NG)
            pool.wait_ge(rows_stored, 16 * NG)

            def load_choices(j, b):
                row = pool.value_load(plan[0:1, 2, bass.ds(j, 1)], min_val=0, max_val=TABLE // TILE - 1)
                pool.dma_start(gmeta[:, b, :, :].rearrange("p k w -> p (k w)"),
                               choice_tiles[bass.ds(row, 1), :, :].rearrange("r p n -> (r p) n")
                               ).then_inc(gmeta_loaded, 16)
                wait_apart(pool, gmeta_loaded, at(j, 16, 16))
                pool.tensor_scalar(gidx[:, b, :], gmeta[:, b, :, 0], NTOK - 1, None, ALU.min).then_inc(gidx_ready, 1)
                wait_apart(pool, gidx_ready, at(j, 1, 1))

            def gather_rows(j, b):
                for k in range(SUB):
                    pool.indirect_dma_start(
                        grow[:, b, k, :], None, token_rows[:, :],
                        bass.IndirectOffsetOnAxis(ap=gidx[:, b, k:k + 1], axis=0)).then_inc(grow_loaded, 16)

            def keep_meta(j, b):
                pool.tensor_copy(smeta[:, b, :, :], gmeta[:, b, :, :]).then_inc(smeta_ready, 1)

            def add_rows(j, b):
                wait_apart(pool, Y_free, at(j, SUB, SUB) + NG * Y_USES)
                for k in range(SUB):
                    pool.indirect_dma_start(
                        out[:, :], bass.IndirectOffsetOnAxis(ap=smeta[:, b, k, 0:1], axis=0),
                        ysb[:, b, k, :], None, compute_op=ALU.add).then_inc(added, 16)

            def tile_steps(j, b, older=2):
                if older >= 2:
                    wait_apart(pool, added, at(j - 1, 16 * SUB, 0))
                keep_meta(j, b)
                pool.wait_ge(smeta_ready, at(j, 1, 1))
                load_choices(j + 2, b)
                wait_apart(pool, T_full, at(j, 1, 1) + NG * T_USES)
                gather_rows(j + 2, b)
                if older >= 1:
                    add_rows(j - 1, 1 - b)

            def last_added(j, b):
                wait_apart(pool, added, at(j - 1, 16 * SUB, 0))
                add_rows(j - 1, 1 - b)
                wait_apart(pool, added, at(j, 16 * SUB, 0))
                wait_apart(pool, grow_loaded, at(j, 16 * SUB, 16 * SUB * 2))

            for b in range(2):
                load_choices(b, b)
                gather_rows(b, b)
                pool.wait_ge(grow_loaded, 16 * SUB * (b + 1))
            tile_steps(0, 0, 0)
            pool.wait_ge(out_stored, 16 * NG)
            tile_steps(1, 1, 1)
            with pool.Fori(1, MIN_T // 2) as i:
                for b in range(2):
                    tile_steps(i * 2 + b, b)
            steps_that_vary(pool, tile_count(pool), tile_steps, last_added)

        @block.scalar
        def _(act):
            act.dma_start(cols[:, :], columns).then_inc(biases_loaded, 16)
            for s in range(2):
                act.dma_start(btok2[:, s, :], b_tok.partition_broadcast(P)).then_inc(biases_loaded, 16)
                act.dma_start(bv2[:, s, :], b_v.partition_broadcast(P)).then_inc(biases_loaded, 16)
            act.wait_ge(biases_loaded, 16 * 5)
            act.activation(unused[:, :], cols[:, 0:1], ACT.Silu)

            def split_high(g, t, first):
                act.wait_ge(stage_loaded, at(g, 48, 16 * (t + 1)))
                if first:
                    dst = W[:, 2 * t * PART:(2 * t + 1) * PART]
                else:
                    act.wait_ge(split_stored, at(g - 1, 48, 16 * t))
                    dst = split[:, 0, :]
                act.activation(dst, stage[:, :], ACT.Copy).then_inc(split_hi, 1)

            def normalise_x(g):
                act.wait_ge(x_moments, at(g, 1, 0))
                for s in range(GS):
                    last = act.activation(xin[0:S, s, :], xin[0:S, s, :], ACT.Identity, bias=x_shift[0:S, s:s + 1],
                                          scale=x_scale[0:S, s:s + 1])
                last.then_inc(xhat_ready, 1)

            def silu_table():
                act.activation(unused[:, :], cols[:, 0:1], ACT.Silu)

            def token_inputs(g, k):
                bank_, full, free, uses, use = X_AT[k]
                act.wait_ge(full, at(g, uses, use + 1))
                act.activation(yT[:, k, :], bank_[:, 0:GT], ACT.Identity, bias=bet[:, k:k + 1],
                               scale=gam[:, k:k + 1]).then_inc(free, 1)

            def xn_high_part(g, k):
                bank_, full, free, uses, use = XN_AT[k]
                act.wait_ge(full, at(g, uses, use + 1))
                act.activation(xn_parts[:, 0, k, :], bank_[:, 0:GT], ACT.Copy).then_inc(xn_high, 1)

            def relu(g, a):
                act.wait_ge(A_free[a], at(g, A_USES[a], A_TOK[a] + 1))
                act.activation(h[0:S, 2 * a:2 * a + 2, :], hpre[0:S, 2 * a:2 * a + 2, :], ACT.Relu
                               ).then_inc(h_ready, 1)

            def normed_T(g, k, where):
                bank_, full, free, uses, use = where[k]
                act.wait_ge(full, at(g, uses, use + 1))
                act.activation(xnT[:, k, :], bank_[:, 0:GT], ACT.Copy).then_inc(free, 1)

            def queries_keys(g, w):
                for m in range(DC):
                    act.wait_ge(A_full[m], at(g, A_USES[m], A_QK[w][m] + 1))
                    act.activation((qT, kT)[w][:, m, :], psA[m][:, 0:GT], ACT.Identity,
                                   bias=bqk[:, w, m:m + 1]).then_inc(A_free[m], 1)

            def exps(g):
                act.wait_ge(smax_ready, at(g, 1, 1))
                for s in range(GS):
                    last = act.activation(prob[0:S, s, :], psT[0:S, s * S:(s + 1) * S], ACT.Exp,
                                          bias=smax[0:S, s:s + 1], scale=D ** -0.5, accum_out=ssum[0:S, s:s + 1])
                last.then_inc(T_free, 1)
                silu_table()

            def probs_T(g):
                act.wait_ge(A_full[0], at(g, A0_USES, A0_PT + 1))
                act.activation(probT[0:S, :, :].rearrange("p s t -> p (s t)"), psA[0][0:S, 0:GT], ACT.Copy
                               ).then_inc(A_free[0], 1)

            def token_rows_high(g):
                act.wait_ge(xn2_ready, at(g, 1, 1))
                act.wait_ge(rows_stored, at(g, 16, 0))
                act.activation(rows[0:S, :, 0:D], xn[0:S, :, :], ACT.Copy).then_inc(rows_hi, 1)

            def ffn_inputs(g):
                for k in range(DC):
                    bank_, full, free, uses, use = H_AT[k]
                    act.wait_ge(full, at(g, uses, use + 1))
                    act.activation(x2T[:, 0, k, :], bank_[:, 0:GT], ACT.Copy).then_inc(x2_hi, 1)

            def router_inputs(g):
                for k in range(DC):
                    act.wait_ge(x2_lo, at(g, DC, k + 1))
                    normed_T(g, k, H_AT)

            def router_T(g):
                act.wait_ge(T_full, at(g, T_USES, T_LT + 1))
                act.activation(logT[:, :], psT[0:E, 0:GT], ACT.Copy).then_inc(T_free, 1)

            def router_exp(g):
                act.wait_ge(Y_free, at(g, Y_USES, Y_LG + 1))
                act.activation(pr[0:S, :, :], lg[0:S, :, :], ACT.Exp).then_inc(e_ready, 1)
                silu_table()

            def ffn_piece(g, c):
                if c < HC:
                    act.wait_ge(G_full[c % 2], at(g, G_USES[c % 2], G_GATE[c % 2] + c // 2 + 1))
                    act.wait_ge(hid_lo, at(g, HC, max(c - 1, 0)))
                    act.activation(sil[:, c % 2, 0:GT], psG[c % 2][:, 0:GT], ACT.Silu).then_inc(G_free[c % 2], 1)
                if c >= 1:
                    act.wait_ge(hf_ready, at(g, HC, c))
                    if c == 1:
                        act.wait_ge(G_full[0], at(g, G_USES[0], 0))
                    act.activation(hid[:, 0, c - 1, 0:GT], sil[:, (c - 1) % 2, 0:GT], ACT.Copy).then_inc(hid_hi, 1)

            def group(g, first=False, later=True):
                ffn = (lambda c: None) if first else (lambda c: ffn_piece(g - 1, c))
                if not first:
                    normalise_x(g)
                token_inputs(g, 0)
                token_inputs(g, 1)
                if not first:
                    ffn_inputs(g - 1)
                token_inputs(g, 2)
                token_inputs(g, 3)
                if not first:
                    router_inputs(g - 1)
                ffn(0)
                if later:
                    split_high(g - 1, 2, False)
                if not first:
                    router_T(g - 1)
                    token_rows_high(g - 1)
                if first:
                    act.wait_ge(consts_loaded, 48)
                    act.activation(wqkv[:, 0, :, :, :], wqkv_staged, ACT.Copy).then_inc(consts_high, 1)
                    split_high(g, 0, first)
                ffn(1)
                if not first:
                    router_exp(g - 1)
                relu(g, 0)
                relu(g, 1)
                ffn(2)
                ffn(3)
                split_high(g, int(first), first)
                ffn(4)
                ffn(5)
                xn_high_part(g, 0)
                xn_high_part(g, 1)
                ffn(6)
                queries_keys(g, 0)
                queries_keys(g, 1)
                ffn(7)
                ffn(8)
                if first:
                    split_high(g, 2, first)
                exps(g)
                probs_T(g)
                if not first:
                    split_high(g, 1, first)

            group(0, first=True, later=False)
            group(1, later=False)
            with act.Fori(2, NG) as g:
                group(g)
            ffn_inputs(NG - 1)
            router_inputs(NG - 1)
            token_rows_high(NG - 1)
            ffn_piece(NG - 1, 0)
            router_T(NG - 1)
            router_exp(NG - 1)
            for c in range(1, HC + 1):
                ffn_piece(NG - 1, c)
            split_high(NG - 1, 2, False)

            def routed_tile(j, b, first):
                Q = HC // 2
                for q in range(Q + 1):
                    if q < Q:
                        act.wait_ge(G_full[q % 2], at(j, Q // 2, q // 2 + 1) + NG * G_USES[q % 2])
                        act.wait_ge(hid_lo, at(j, Q, max(q - 1, 0)) + NG * HC)
                        act.activation(sil[:, q % 2, :], psG[q % 2][:, :], ACT.Silu).then_inc(G_free[q % 2], 1)
                    if q >= 1:
                        act.wait_ge(hf_ready, at(j, Q, q) + NG * HC)
                        if q == 1 and first:
                            act.wait_ge(G_full[0], NG * G_USES[0])
                        elif q == 1:
                            act.wait_ge(Y_full, (j - 1) * SUB + NG * Y_USES)
                        act.activation(hidr[:, b, 0, 2 * q - 2:2 * q, :],
                                       sil[:, (q - 1) % 2, :].rearrange("p (c t) -> p c t", c=2),
                                       ACT.Copy).then_inc(hid_hi, 1)

            for b in range(2):
                routed_tile(b, b, True)
            with act.Fori(1, MIN_T // 2) as i:
                for b in range(2):
                    routed_tile(i * 2 + b, b, False)
            steps_that_vary(act, tile_count(act), lambda j, b: routed_tile(j, b, False))

        @block.vector
        def _(vec):
            NORM_STEPS, ROUTE_STEPS = 13, 29
            kinds = {"x norm": (x_step, NORM_STEPS), "attention": (dve_step, 2 * NORM_STEPS + 2),
                     "routing": (route_step, ROUTE_STEPS),
                     "plan": (plan_step, None)}
            state = {}

            def begin(kind, g):
                sem, steps = kinds[kind]
                state.update(sem=sem, g=g, steps=steps, n=0)

            def end():
                assert state["n"] == state["steps"], state

            def link(ins, wait=lambda eng, sem, value: eng.wait_ge(sem, value)):
                state["n"] += 1
                ins.then_inc(state["sem"], 1)
                wait(vec, state["sem"], at(state["g"], state["steps"] or 0, state["n"]))

            def bc(ap, n):
                return ap.unsqueeze(2).to_broadcast([S, GS, n])

            def norm(src, dst, done):
                statistics(src)
                moments()
                normalise(src, dst, done)

            def statistics(src, ready=lambda s: None):
                for s in range(GS):
                    ready(s)
                    last = vec.bn_stats(stats[0:S, s, :], src[0:S, s, :])
                link(last, wait_apart)

            def moments():
                for s in range(GS):
                    last = vec.bn_aggr(mv[0:S, s, :], stats[0:S, s, :])
                link(last)
                link(vec.tensor_scalar(ve[0:S, :], mv[0:S, :, 1], EPS, None, ALU.add))
                vec.tensor_scalar(hv[0:S, :], ve[0:S, :], -0.5, None, ALU.mult)
                link(vec.tensor_scalar(rs[0:S, :].bitcast(I32), ve[0:S, :].bitcast(I32), -0.5, RSQRT_SEED,
                                       ALU.mult, ALU.add))
                for _ in range(3):
                    link(vec.tensor_tensor(sq[0:S, :], rs[0:S, :], rs[0:S, :], ALU.mult))
                    link(vec.tensor_tensor(sq[0:S, :], sq[0:S, :], hv[0:S, :], ALU.mult))
                    link(vec.scalar_tensor_tensor(rs[0:S, :], sq[0:S, :], 1.5, rs[0:S, :], ALU.add, ALU.mult))

            def normalise(src, dst, done):
                for s in range(GS):
                    last = vec.tensor_scalar(dst[0:S, s, :], src[0:S, s, :], mv[0:S, s, 0:1], rs[0:S, s:s + 1],
                                             ALU.subtract, ALU.mult)
                last.then_inc(done, 1)

            def norm_x(g, first=False):
                begin("x norm", g)
                vec.wait_ge(x_loaded, at(g, 16, 16))
                statistics(xin)
                moments()
                if first:
                    normalise(xin, xin, xhat_ready)
                    return end()
                vec.tensor_copy(x_scale[0:S, :], rs[0:S, :])
                vec.scalar_tensor_tensor(x_shift[0:S, :], mv[0:S, :, 0], -1.0, rs[0:S, :], ALU.mult, ALU.mult
                                         ).then_inc(x_moments, 1)
                end()

            def split_low(g, t, first):
                vec.wait_ge(split_hi, at(g, 3, t + 1))
                if first:
                    hi = W[:, 2 * t * PART:(2 * t + 1) * PART]
                    lo = W[:, (2 * t + 1) * PART:(2 * t + 2) * PART]
                else:
                    hi, lo = split[:, 0, :], split[:, 1, :]
                vec.tensor_tensor(lo, stage[:, :], hi, ALU.subtract).then_inc(split_lo, 1)

            def project_bias(g, a):
                vec.wait_ge(A_full[a], at(g, A_USES[a], A_TOK[a] + 1))
                if a == 0:
                    vec.wait_ge(hres_ready, at(g, 1, 0))
                vec.tensor_tensor(hpre[0:S, 2 * a:2 * a + 2, :].rearrange("p s d -> p (s d)"),
                                  psA[a][0:S, :], btok2[0:S, :, :].rearrange("p s d -> p (s d)"),
                                  ALU.add).then_inc(A_free[a], 1)

            def values(g):
                for a in range(2):
                    vec.wait_ge(A_full[a], at(g, A_USES[a], A_V[a] + 1))
                    vec.tensor_tensor(v[0:S, 2 * a:2 * a + 2, :].rearrange("p s d -> p (s d)"),
                                      psA[a][0:S, :], bv2[0:S, :, :].rearrange("p s d -> p (s d)"),
                                      ALU.add).then_inc(A_free[a], 1)

            def score_max(g):
                vec.wait_ge(T_full, at(g, T_USES, T_SC + 1))
                link(vec.tensor_reduce(smax[0:S, :], psT[0:S, 0:GT].rearrange("p (s t) -> p s t", s=GS),
                                       AX, ALU.max))
                vec.tensor_scalar(smax[0:S, :], smax[0:S, :], -D ** -0.5, None, ALU.mult).then_inc(smax_ready, 1)

            def prob_sums(g):
                vec.wait_ge(T_free, at(g, T_USES, T_SC + 1))
                link(vec.reciprocal(ssum[0:S, :], ssum[0:S, :]))

            def attended(g):
                for a in (1, 0):
                    vec.wait_ge(A_full[a], at(g, A_USES[a], A_PV[a] + 1))
                    for i in range(2):
                        s = 2 * (1 - a) + i
                        last = vec.scalar_tensor_tensor(h2[0:S, s, :], psA[a][0:S, i * D:(i + 1) * D],
                                                        ssum[0:S, s:s + 1], h[0:S, s, :], ALU.mult, ALU.add)
                    last.then_inc(A_free[a], 1)
                vec.wait_ge(A_free[0], at(g, A0_USES, A0_PV + 1))

            def token_rows_low(g):
                vec.wait_ge(rows_hi, at(g, 1, 1))
                vec.tensor_tensor(rows[0:S, :, D:2 * D], xn[0:S, :, :], rows[0:S, :, 0:D], ALU.subtract
                                  ).then_inc(rows_lo, 1)

            def ffn_inputs_low(g):
                for k in range(DC):
                    vec.wait_ge(x2_hi, at(g, DC, k + 1))
                    vec.tensor_tensor(x2T[:, 1, k, :], H_AT[k][0][:, 0:GT], x2T[:, 0, k, :], ALU.subtract
                                      ).then_inc(x2_lo, 1)

            top2_steps = [0]

            def router_logits(g):
                begin("routing", g)
                vec.wait_ge(Y_full, at(g, Y_USES, Y_LG + 1))
                logits = psY[0:S, 0:GS * 8].rearrange("p (s e) -> p s e", e=8)[:, :, 0:E]
                link(vec.tensor_reduce(m1[0:S, :], logits, AX, ALU.max))
                vec.tensor_tensor(lg[0:S, :, :], logits, bc(m1[0:S, :], E), ALU.subtract).then_inc(Y_free, 1)

            def top2(g):
                begin("routing", g)
                state["n"] = 1
                vec.wait_ge(e_ready, at(g, 1, 1))
                link(vec.tensor_reduce(r1[0:S, :], pr[0:S, :, :], AX, ALU.add))
                link(vec.reciprocal(r1[0:S, :], r1[0:S, :]))
                link(vec.tensor_tensor(pr[0:S, :, :], pr[0:S, :, :], bc(r1[0:S, :], E), ALU.mult))
                prio_bc = prio[0:S, :].unsqueeze(1).to_broadcast([S, GS, E])
                for top, hot in ((m1, oh1), (m2, oh2)):
                    link(vec.tensor_reduce(top[0:S, :], pr[0:S, :, :], AX, ALU.max))
                    link(vec.tensor_tensor(t7[0:S, :, :], pr[0:S, :, :], bc(top[0:S, :], E), ALU.is_equal))
                    link(vec.tensor_tensor(t7[0:S, :, :], t7[0:S, :, :], prio_bc, ALU.mult))
                    link(vec.tensor_reduce(r1[0:S, :], t7[0:S, :, :], AX, ALU.max))
                    link(vec.tensor_tensor(hot[0:S, :, :], prio_bc, bc(r1[0:S, :], E), ALU.is_equal))
                    if hot is oh1:
                        link(vec.scalar_tensor_tensor(pr[0:S, :, :], oh1[0:S, :, :], -2.0, pr[0:S, :, :],
                                                      ALU.mult, ALU.add))
                vec.tensor_tensor(pick[0:S, :, :], oh1[0:S, :, :], oh2[0:S, :, :], ALU.add).then_inc(pick_ready, 1)
                link(vec.tensor_tensor(r1[0:S, :], m1[0:S, :], m2[0:S, :], ALU.add))
                link(vec.tensor_scalar(r1[0:S, :], r1[0:S, :], 1e-9, None, ALU.add))
                link(vec.reciprocal(r1[0:S, :], r1[0:S, :]))
                vec.wait_ge(meta_stored, at(g, 16 * 2 * GS, 0))
                meta_f = meta[0:S, :, :, :].bitcast(F32)
                for k, top in enumerate((m1, m2)):
                    vec.tensor_tensor(meta_f[:, :, k, 1], top[0:S, :], r1[0:S, :], ALU.mult)
                    last = vec.tensor_copy(meta[0:S, :, k, 0], tokid[0:S, :])
                link(last)
                link(vec.tensor_scalar(tokid[0:S, :], tokid[0:S, :], float(GT), None, ALU.add))
                top2_steps[0] = state["n"]

            def places(g):
                begin("routing", g)
                state["n"] = top2_steps[0]
                vec.wait_ge(Y_full, at(g, Y_USES, Y_RANK + 1))
                rank = psY[0:S, 0:GS * E].rearrange("p (s e) -> p s e", e=E)
                for s in range(GS):
                    link(vec.tensor_tensor(run[0:S, s + 1, :], run[0:S, s, :],
                                           psY[0:S, 64 + s * E:64 + (s + 1) * E], ALU.add))
                vec.tensor_tensor(t7[0:S, :, :], rank, run[0:S, 0:GS, :], ALU.add).then_inc(Y_free, 1)
                vec.wait_ge(Y_free, at(g, Y_USES, Y_RANK + 1))
                for k, hot in enumerate((oh1, oh2)):
                    link(vec.tensor_tensor(hot[0:S, :, :], hot[0:S, :, :], t7[0:S, :, :], ALU.mult))
                    link(vec.tensor_reduce(posf[0:S, :, k], hot[0:S, :, :], AX, ALU.add))
                vec.tensor_copy(pos[0:S, :, :], posf[0:S, :, :]).then_inc(meta_ready, 1)
                link(vec.tensor_copy(run[0:S, 0, :], run[0:S, GS, :]))
                end()

            def ffn_piece(g, c):
                if c < HC:
                    vec.wait_ge(G_free[c % 2], at(g, G_USES[c % 2], G_GATE[c % 2] + c // 2 + 1))
                    vec.wait_ge(U_full[c % 2], at(g, U_USES, c // 2 + 1))
                    vec.tensor_tensor(sil[:, c % 2, 0:GT], psU[c % 2][:, 0:GT], sil[:, c % 2, 0:GT], ALU.mult
                                      ).then_inc(hf_ready, 1)
                if c >= 1:
                    vec.wait_ge(hid_hi, at(g, HC, c))
                    vec.tensor_tensor(hid[:, 1, c - 1, 0:GT], sil[:, (c - 1) % 2, 0:GT], hid[:, 0, c - 1, 0:GT],
                                      ALU.subtract).then_inc(hid_lo, 1)

            def ffn_out(g, s):
                vec.wait_ge(hres_ready, at(g, 1, 1))
                if s == 0:
                    vec.wait_ge(out_stored, at(g, 16, 0))
                src, full, free, uses, use = DOWN_AT[s]
                vec.wait_ge(full, at(g, uses, use + 1))
                vec.tensor_tensor(yout[0:S, s, :], src[0:S, 0:D], hres[0:S, s, :], ALU.add).then_inc(free, 1)

            def group(g, first=False, later=True, last=False):
                ffn = (lambda c: None) if first else (lambda c: ffn_piece(g - 1, c))
                down = (lambda s: None) if first else (lambda s: ffn_out(g - 1, s))
                if not first:
                    ffn_inputs_low(g - 1)
                ffn(0)
                if later:
                    split_low(g - 1, 2, False)
                if not first:
                    token_rows_low(g - 1)
                ffn(1)
                if not first:
                    router_logits(g - 1)
                    top2(g - 1)
                if first:
                    vec.wait_ge(consts_high, 1)
                    vec.tensor_tensor(wqkv[:, 1, :, :, :], wqkv_staged, wqkv[:, 0, :, :, :], ALU.subtract
                                      ).then_inc(consts_low, 1)
                    split_low(g, 0, first)
                project_bias(g, 0)
                project_bias(g, 1)
                begin("attention", g)
                statistics(h, lambda s: vec.wait_ge(h_ready, at(g, 2, s // 2 + 1)) if s % 2 == 0 else None)
                ffn(2)
                moments()
                ffn(3)
                normalise(h, xn, xn_ready)
                ffn(4)
                ffn(5)
                xn_low_part(g, 0)
                xn_low_part(g, 1)
                split_low(g, int(first), first)
                ffn(6)
                if not last:
                    norm_x(g + 1)
                ffn(7)
                ffn(8)
                resume(g)
                score_max(g)
                values(g)
                if not first:
                    places(g - 1)
                if first:
                    split_low(g, 2, first)
                resume(g, 1)
                prob_sums(g)
                if not first:
                    split_low(g, 1, first)
                down(0)
                attended(g)
                norm(h2, xn, xn2_ready)
                end()
                for s in range(1, GS):
                    down(s)

            def resume(g, more=0):
                begin("attention", g)
                state["n"] = NORM_STEPS + more

            def xn_low_part(g, k):
                bank_, full, free, uses, use = XN_AT[k]
                vec.wait_ge(xn_high, at(g, DC, k + 1))
                vec.tensor_tensor(xn_parts[:, 1, k, :], bank_[:, 0:GT], xn_parts[:, 0, k, :], ALU.subtract
                                  ).then_inc(free, 1)

            norm_x(0, first=True)
            vec.wait_ge(iota_made, 5)
            vec.tensor_scalar(padfill[:, :, 0], padfill[:, :, 0], TILE - 1, None, ALU.bitwise_and
                              ).then_inc(pads_masked, 1)
            vec.wait_ge(pads_masked, 1)
            vec.tensor_scalar(padfill[:, :, 0], padfill[:, :, 0], NTOK, None, ALU.add).then_inc(pads_made, 1)
            vec.tensor_copy(prio[:, :], iota_i[:, 0:E])
            vec.tensor_copy(base_e[:, :], iota_i[:, 8:8 + E])
            vec.tensor_copy(run[:, 0, :], iota_i[:, 8:8 + E])
            vec.tensor_copy(tokid[:, :], iota_i[:, 16:16 + GS])
            vec.tensor_copy(tile_no[:, :], iota_i[:, 20:20 + PLANNED]).then_inc(indices_made, 1)
            vec.wait_ge(indices_made, 1)
            vec.wait_ge(biases_loaded, 16 * 5)
            group(0, first=True, later=False)
            group(1, later=False)
            with vec.Fori(2, NG - 1) as g:
                group(g)
            group(NG - 1, last=True)
            ffn_inputs_low(NG - 1)
            token_rows_low(NG - 1)
            ffn_piece(NG - 1, 0)
            router_logits(NG - 1)
            top2(NG - 1)
            ffn_piece(NG - 1, 1)
            places(NG - 1)

            def count_tiles():
                begin("plan", 0)
                link(vec.tensor_tensor(tcount[:, :], run[0:1, 0, :], base_e[0:1, :], ALU.subtract))
                link(vec.tensor_scalar(tcount[:, :], tcount[:, :], float(TILE - 1), None, ALU.add))
                link(vec.tensor_copy(ntile[:, :], tcount[:, :]))
                link(vec.tensor_scalar(ntile[:, :], ntile[:, :], TILE.bit_length() - 1, None,
                                       ALU.logical_shift_right))
                link(vec.tensor_copy(tcount[:, :], ntile[:, :]))
                link(vec.tensor_copy(tends[:, 0:1], tcount[:, 0:1]))

            def end_tiles():
                for e in range(1, E):
                    link(vec.tensor_tensor(tends[:, e:e + 1], tends[:, e - 1:e], tcount[:, e:e + 1], ALU.add))
                vec.tensor_copy(ends_i[:, 0:E], tends[:, :])

            def table_rows():
                link(vec.tensor_tensor(passed[:, :, :], tile_no[0:1, :].unsqueeze(2).to_broadcast([1, PLANNED, E]),
                                       tends[:, :].unsqueeze(1).to_broadcast([1, PLANNED, E]), ALU.is_ge))
                link(vec.tensor_reduce(ej[:, :], passed[:, :, 0:E - 1], AX, ALU.add))
                link(vec.tensor_tensor(passed[:, :, :], passed[:, :, :],
                                       tcount[:, :].unsqueeze(1).to_broadcast([1, PLANNED, E]), ALU.mult))
                link(vec.tensor_reduce(sj[:, :], passed[:, :, 0:E - 1], AX, ALU.add))
                link(vec.tensor_tensor(sj[:, :], tile_no[0:1, :], sj[:, :], ALU.subtract))
                link(vec.scalar_tensor_tensor(sj[:, :], ej[:, :], float(REGION // TILE), sj[:, :],
                                              ALU.mult, ALU.add))
                vec.tensor_copy(plan[:, 2, :], sj[:, :]).then_inc(rows_planned, 1)

            def ring_slots():
                link(vec.tensor_scalar(ej[:, :], ej[:, :], 1.0, None, ALU.add))
                vec.tensor_scalar(plan[:, 1, :], ej[:, :], 16.0, None, ALU.mult)
                for n in range(NS, NE, NS):
                    link(vec.tensor_scalar(tj[:, :], ej[:, :], float(NS), float(-NS), ALU.is_ge, ALU.mult))
                    link(vec.tensor_tensor(ej[:, :], ej[:, :], tj[:, :], ALU.add))
                vec.tensor_scalar(plan[:, 0, :], ej[:, :], float(SLOT), None, ALU.mult).then_inc(plan_ready, 1)

            ffn_piece(NG - 1, 2)
            count_tiles()
            ffn_piece(NG - 1, 3)
            end_tiles()
            ffn_piece(NG - 1, 4)
            table_rows()
            for c in range(5, HC + 1):
                ffn_piece(NG - 1, c)
            ring_slots()
            ffn_out(NG - 1, 0)
            split_low(NG - 1, 2, False)
            for s in range(1, GS):
                ffn_out(NG - 1, s)

            def tile_T(j, b):
                vec.wait_ge(T_full, at(j, 1, 1) + NG * T_USES)
                vec.tensor_copy(gxT[:, b, :, :, :].rearrange("p a k t -> p (a k t)"), psT_b).then_inc(T_free, 1)

            def tile_piece(j, b, q):
                Q = HC // 2
                if q < Q:
                    vec.wait_ge(G_free[q % 2], at(j, Q // 2, q // 2 + 1) + NG * G_USES[q % 2])
                    vec.wait_ge(U_full[q % 2], at(j, Q // 2, q // 2 + 1) + NG * U_USES)
                    vec.tensor_tensor(sil[:, q % 2, :], psU[q % 2][:, :], sil[:, q % 2, :], ALU.mult
                                      ).then_inc(hf_ready, 1)
                if q >= 1:
                    vec.wait_ge(hid_hi, at(j, Q, q) + NG * HC)
                    vec.tensor_tensor(hidr[:, b, 1, 2 * q - 2:2 * q, :],
                                      sil[:, (q - 1) % 2, :].rearrange("p (c t) -> p c t", c=2),
                                      hidr[:, b, 0, 2 * q - 2:2 * q, :], ALU.subtract).then_inc(hid_lo, 1)

            def tile_out(j, b, k):
                vec.wait_ge(Y_full, at(j, SUB, k + 1) + NG * Y_USES)
                vec.wait_ge(smeta_ready, at(j, 1, 1))
                vec.tensor_scalar(ysb[:, b, k, :], psY[:, 0:D], smeta[:, b, k, 1:2].bitcast(F32), None, ALU.mult
                                  ).then_inc(Y_free, 1)

            def routed_tile(j, b, older=True):
                tile_piece(j, b, 0)
                tile_piece(j, b, 1)
                if older:
                    tile_out(j - 1, 1 - b, 0)
                tile_piece(j, b, 2)
                tile_T(j + 1, 1 - b)
                tile_piece(j, b, 3)
                tile_piece(j, b, 4)
                if older:
                    tile_out(j - 1, 1 - b, 1)

            def last_out(j, b):
                for k in range(SUB):
                    tile_out(j - 1, 1 - b, k)

            tile_T(0, 0)
            routed_tile(0, 0, older=False)
            routed_tile(1, 1)
            with vec.Fori(1, MIN_T // 2) as i:
                for b in range(2):
                    routed_tile(i * 2 + b, b)
            steps_that_vary(vec, tile_count(vec), routed_tile, last_out)

        @block.tensor
        def _(pe):
            pe.wait_ge(masks_made, 6)
            pe.wait_ge(consts_loaded, 48)

            def transposes(g, where, src):
                bank_, full, free, uses, use = where
                pe.wait_ge(free, at(g, uses, use))
                for s in range(GS):
                    last = pe.transpose(bank_[:, s * S:(s + 1) * S], src(s), ident[0:S, 0:S])
                last.then_inc(full, 1)

            def written(g, where):
                for bank_, full, free, uses, use in where:
                    pe.wait_ge(free, at(g, uses, use + 1))

            def x_T(g, k):
                transposes(g, X_AT[k], lambda s: xin[0:S, s, k * P:(k + 1) * P])

            def xn_T(g, k, where):
                transposes(g, where[k], lambda s: xn[0:S, s, k * P:(k + 1) * P])

            def normed_tokens_T(g):
                pe.wait_ge(xn2_ready, at(g, 1, 1))
                xn_T(g, 0, H_AT)
                xn_T(g, 1, H_AT)

            def project(g):
                written(g, X_AT)
                for a in range(2):
                    pe.wait_ge(A_free[a], at(g, A_USES[a], A_TOK[a]))
                    for i in range(2):
                        s = 2 * a + i
                        for k in range(FC):
                            last = pe.matmul(psA[a][0:S, i * D:(i + 1) * D], yT[:, k, s * S:(s + 1) * S],
                                             wtok[:, k, :], start=(k == 0), stop=(k == FC - 1))
                    last.then_inc(A_full[a], 1)

            def queries_keys(g, w):
                if w == 0:
                    written(g, XN_AT)
                    pe.wait_ge(consts_low, 1)
                for m in range(DC):
                    pe.wait_ge(A_free[m], at(g, A_USES[m], A_QK[w][m]))
                    n = 0
                    for wp, xp in TERMS:
                        for k in range(DC):
                            last = pe.matmul(psA[m][:, 0:GT], wqkv[:, wp, w, k, m * P:(m + 1) * P],
                                             xn_parts[:, xp, k, :], start=(n == 0), stop=(n == 3 * DC - 1))
                            n += 1
                    last.then_inc(A_full[m], 1)

            def values(g):
                for a in range(2):
                    pe.wait_ge(A_free[a], at(g, A_USES[a], A_V[a]))
                    for i in range(2):
                        s = 2 * a + i
                        n = 0
                        for wp, xp in TERMS:
                            for k in range(DC):
                                last = pe.matmul(psA[a][0:S, i * D:(i + 1) * D],
                                                 xn_parts[:, xp, k, s * S:(s + 1) * S], wqkv[:, wp, 2, k, :],
                                                 start=(n == 0), stop=(n == 3 * DC - 1))
                                n += 1
                    last.then_inc(A_full[a], 1)

            def scores(g):
                for m in range(DC):
                    pe.wait_ge(A_free[m], at(g, A_USES[m], A_QK[1][m] + 1))
                pe.wait_ge(T_free, at(g, T_USES, T_SC))
                for s in range(GS):
                    for m in range(DC):
                        last = pe.matmul(psT[0:S, s * S:(s + 1) * S], qT[:, m, s * S:(s + 1) * S],
                                         kT[:, m, s * S:(s + 1) * S], start=(m == 0), stop=(m == DC - 1))
                last.then_inc(T_full, 1)

            def probs_T(g):
                pe.wait_ge(T_free, at(g, T_USES, T_SC + 1))
                pe.wait_ge(A_free[0], at(g, A0_USES, A0_PT))
                for s in range(GS):
                    last = pe.transpose(psA[0][0:S, s * S:(s + 1) * S], prob[0:S, s, :], ident[0:S, 0:S])
                last.then_inc(A_full[0], 1)

            def attend(g):
                pe.wait_ge(A_free[0], at(g, A0_USES, A0_PT + 1))
                for a in (1, 0):
                    pe.wait_ge(A_free[a], at(g, A_USES[a], A_PV[a]))
                    for i in range(2):
                        s = 2 * (1 - a) + i
                        last = pe.matmul(psA[a][0:S, i * D:(i + 1) * D], probT[0:S, s, :], v[0:S, s, :],
                                         start=True, stop=True)
                    last.then_inc(A_full[a], 1)

            def router(g):
                written(g, H_AT)
                pe.wait_ge(T_free, at(g, T_USES, T_LT))
                for k in range(DC):
                    last = pe.matmul(psT[0:E, 0:GT], wrt[:, k, :], xnT[:, k, :], start=(k == 0),
                                     stop=(k == DC - 1))
                last.then_inc(T_full, 1)

            def logits(g):
                pe.wait_ge(T_free, at(g, T_USES, T_LT + 1))
                wait_apart(pe, Y_free, at(g, Y_USES, Y_LG))
                for s in range(GS):
                    last = pe.transpose(psY[0:S, s * 8:s * 8 + E], logT[:, s * S:(s + 1) * S], ident[0:E, 0:E])
                last.then_inc(Y_full, 1)

            def ranks(g):
                pe.wait_ge(pick_ready, at(g, 1, 1))
                pe.wait_ge(Y_free, at(g, Y_USES, Y_RANK))
                picks = pick[0:S, :, :].rearrange("p s e -> p (s e)")
                pe.matmul(psY[0:S, 0:GS * E], before[0:S, 0:S], picks, start=True, stop=True)
                pe.matmul(psY[0:S, 64:64 + GS * E], ones_b[0:S, 0:S], picks, start=True, stop=True
                          ).then_inc(Y_full, 1)

            def ffn_piece(g, c):
                if c == 0:
                    pe.wait_ge(x2_hi, at(g, DC, DC))
                    pe.wait_ge(x2_lo, at(g, DC, DC))
                for which, ps, full in ((0, psG, G_full), (1, psU, U_full)):
                    if which == 0:
                        pe.wait_ge(G_free[c % 2], at(g, G_USES[c % 2], G_GATE[c % 2] + c // 2))
                    else:
                        pe.wait_ge(hf_ready, at(g, HC, max(c - 1, 0)))
                    n = 0
                    for wp, xp in TERMS:
                        for k in range(DC):
                            last = pe.matmul(ps[c % 2][:, 0:GT], wcols(0, which, wp, k * DFF + c * P, P),
                                             x2T[:, xp, k, :], start=(n == 0), stop=(n == 3 * DC - 1))
                            n += 1
                    last.then_inc(full[c % 2], 1)

            def ffn_down(g, s):
                if s == 0:
                    pe.wait_ge(hid_hi, at(g, HC, HC))
                    pe.wait_ge(hid_lo, at(g, HC, HC))
                dst, full, free, uses, use = DOWN_AT[s]
                pe.wait_ge(free, at(g, uses, use))
                n = 0
                for wp, xp in TERMS:
                    for c in range(HC):
                        last = pe.matmul(dst[0:S, 0:D], hid[:, xp, c, s * S:(s + 1) * S],
                                         wcols(0, 2, wp, c * D, D), start=(n == 0), stop=(n == 3 * HC - 1))
                        n += 1
                last.then_inc(full, 1)

            def group(g, first=False):
                ffn = (lambda c: None) if first else (lambda c: ffn_piece(g - 1, c))
                down = (lambda s: None) if first else (lambda s: ffn_down(g - 1, s))
                pe.wait_ge(xhat_ready, at(g, 1, 1))
                x_T(g, 0)
                x_T(g, 1)
                if not first:
                    normed_tokens_T(g - 1)
                x_T(g, 2)
                x_T(g, 3)
                ffn(0)
                if not first:
                    router(g - 1)
                ffn(1)
                if not first:
                    logits(g - 1)
                project(g)
                for c in range(2, 6):
                    ffn(c)
                pe.wait_ge(xn_ready, at(g, 1, 1))
                xn_T(g, 0, XN_AT)
                xn_T(g, 1, XN_AT)
                ffn(6)
                queries_keys(g, 0)
                queries_keys(g, 1)
                ffn(7)
                if not first:
                    ranks(g - 1)
                scores(g)
                values(g)
                probs_T(g)
                down(0)
                attend(g)
                for s in range(1, GS):
                    down(s)

            group(0, True)
            pe.wait_ge(split_lo, 3)
            group(1)
            with pe.Fori(2, NG) as g:
                group(g)
            normed_tokens_T(NG - 1)
            ffn_piece(NG - 1, 0)
            router(NG - 1)
            logits(NG - 1)
            for c in range(1, HC):
                ffn_piece(NG - 1, c)
                if c == 2:
                    ranks(NG - 1)
            for s in range(GS):
                ffn_down(NG - 1, s)

            pe.wait_ge(plan_ready, 1)

            def tile_T(j, b):
                pe.wait_ge(grow_loaded, at(j, 16 * SUB, 16 * SUB))
                pe.wait_ge(T_free, at(j, 1, 0) + NG * T_USES)
                for a in range(2):
                    for k in range(DC):
                        for r in range(SUB):
                            last = pe.transpose(psT_b[:, ((a * DC + k) * SUB + r) * P:((a * DC + k) * SUB + r + 1) * P],
                                                grow[:, b, r, (a * DC + k) * P:(a * DC + k + 1) * P], ident_b[:, :])
                last.then_inc(T_full, 1)

            def tile_piece(j, b, q, slot_at):
                Q = HC // 2
                if q == 0:
                    pe.wait_ge(T_free, at(j, 1, 1) + NG * T_USES)
                for which, ps, full in ((0, psG, G_full), (1, psU, U_full)):
                    if which == 0:
                        pe.wait_ge(G_free[q % 2], at(j, Q // 2, q // 2) + NG * G_USES[q % 2])
                    else:
                        pe.wait_ge(hf_ready, at(j, Q, max(q - 1, 0)) + NG * HC)
                    for i in range(2):
                        c = 2 * q + i
                        n = 0
                        for wp, xp in TERMS:
                            for k in range(DC):
                                last = pe.matmul(ps[q % 2][:, i * TILE:(i + 1) * TILE],
                                                 wcols(slot_at, which, wp, k * DFF + c * P, P),
                                                 gxT[:, b, xp, k, :], start=(n == 0), stop=(n == 3 * DC - 1))
                                n += 1
                    last.then_inc(full[q % 2], 1)

            def tile_down(j, b, r, slot_at):
                if r == 0:
                    pe.wait_ge(hid_hi, at(j, HC // 2, HC // 2) + NG * HC)
                    pe.wait_ge(hid_lo, at(j, HC // 2, HC // 2) + NG * HC)
                pe.wait_ge(Y_free, at(j, SUB, r) + NG * Y_USES)
                n = 0
                for wp, xp in TERMS:
                    for c in range(HC):
                        last = pe.matmul(psY[:, 0:D], hidr[:, b, xp, c, r * P:(r + 1) * P],
                                         wcols(slot_at, 2, wp, c * D, D), start=(n == 0), stop=(n == 3 * HC - 1))
                        n += 1
                last.then_inc(Y_full, 1)

            def slot_of(j):
                return pe.value_load(plan[0:1, 0, bass.ds(j, 1)], min_val=0, max_val=(NS - 1) * SLOT)

            def planned(j):
                return pe.value_load(plan[0:1, 1, bass.ds(j, 1)], min_val=16, max_val=16 * E), slot_of(j)

            def routed_tile(j, b, older=True, of_tile=None, of_last=None, ahead=False):
                of_tile = of_tile or planned(j)
                loads, here = of_tile
                of_next = None
                pe.wait_ge(expert_loaded, loads)
                tile_piece(j, b, 0, here)
                tile_piece(j, b, 1, here)
                if older:
                    there = of_last[1] if of_last else slot_of(j - 1)
                    tile_down(j - 1, 1 - b, 0, there)
                tile_piece(j, b, 2, here)
                tile_T(j + 1, 1 - b)
                if ahead:
                    of_next = planned(j + 1)
                tile_piece(j, b, 3, here)
                if older:
                    tile_down(j - 1, 1 - b, 1, there)
                return of_tile, of_next

            def last_down(j, b):
                for r in range(SUB):
                    tile_down(j - 1, 1 - b, r, slot_of(j - 1))

            def four_tiles(first, older=True):
                of_last = of_tile = None
                for n in range(4):
                    of_last, of_tile = routed_tile(first + n, n % 2, older=older or n > 0, of_tile=of_tile,
                                                   of_last=of_last, ahead=(n < 3))

            tile_T(0, 0)
            four_tiles(0, older=False)
            with pe.Fori(1, MIN_T // 4) as i:
                four_tiles(i * 4)
            steps_that_vary(pe, tile_count(pe), routed_tile, last_down)


def kernel(**inputs):
    import numpy as np
    import concourse.bacc as bacc
    from concourse.bass_utils import run_bass_kernel_spmd

    a = {k: np.asarray(t) for k, t in inputs.items()}

    def ffn_layout(gate, up, down):
        return np.stack([w.T.reshape(-1, P, w.shape[0]).transpose(1, 0, 2).reshape(P, -1)
                         for w in (gate, up, down)])

    ffn = [ffn_layout(a["L0_ffn_shared_gate"], a["L0_ffn_shared_up"], a["L0_ffn_shared_down"])]
    for e in range(E):
        ffn.append(ffn_layout(a["L0_ffn_routed_gate"][e], a["L0_ffn_routed_up"][e], a["L0_ffn_routed_down"][e]))
    arrays = {
        "in_x": a["x"].reshape(B, S, FAN),
        "in_columns": np.concatenate([a[k].reshape(-1, P).T for k in (
            "L0_tok_ln_gamma", "L0_tok_ln_beta", "L0_attn_b_q", "L0_attn_b_k")], axis=1),
        "in_w_tok": np.ascontiguousarray(a["L0_tok_W"].T),
        "in_b_tok": a["L0_tok_b"],
        "in_w_qkv": np.stack([a["L0_attn_W_q"], a["L0_attn_W_k"], a["L0_attn_W_v"]]),
        "in_b_v": a["L0_attn_b_v"],
        "in_w_ffn": np.stack(ffn),
        "in_w_router": np.ascontiguousarray(a["L0_ffn_router_w"].T),
    }
    nc = bacc.Bacc("TRN2", target_bir_lowering=False, num_devices=1)
    args = [nc.dram_tensor(n, t.shape, mybir.dt.from_np(t.dtype), kind="ExternalInput").ap()
            for n, t in arrays.items()]
    out = nc.dram_tensor("out", (NTOK + TILE, D), F32, kind="ExternalOutput").ap()
    audio_tower(nc, *args, out)
    r = run_bass_kernel_spmd(nc, [arrays], core_ids=[0])
    return r.results[0]["out"][:NTOK].reshape(B, S, D)
```
